# Optimizing a Trainium2 kernel written in Bass

```python
import numpy as np
import jax
import jax.numpy as jnp

def _softmax(x, axis=-1):
    return jax.nn.softmax(x, axis=axis)

def _gelu(x):
    return jax.nn.gelu(x, approximate=True)

def _silu(x):
    return jax.nn.silu(x)

def _sigmoid(x):
    return jax.nn.sigmoid(x)

def _layernorm(x, axis=-1, eps=1e-05):
    m = jnp.mean(x, axis=axis, keepdims=True)
    v = jnp.var(x, axis=axis, keepdims=True)
    return (x - m) / jnp.sqrt(v + eps)

def _scatter_add(tgt, idx, src, axis=0):
    return tgt.at[idx].add(src)

def _segment_sum(src, seg, n):
    return jax.ops.segment_sum(src, seg, n)
kernel_name = 'mk_seq_preln_d1_jaxref_r8_6ce528'

def setup_inputs(seed: int=0):
    np.random.seed(seed)
    _w = jnp.asarray

    def _L0_attn_setup():
        import jax, jax.numpy as jnp
        import numpy as np
        key = jax.random.key(seed)
        ks = jax.random.split(key, 5)
        B, S, D = (1, 512, 256)
        H, Dh = (16, 128)
        scale = 1.0 / np.sqrt(D).astype(np.float32)
        return {'x': jax.random.normal(ks[0], (B, S, D), dtype=jnp.float32), 'W_K': jax.random.normal(ks[1], (H, Dh, D), dtype=jnp.float32) * scale, 'W_Q': jax.random.normal(ks[2], (H, Dh, D), dtype=jnp.float32) * scale, 'W_V': jax.random.normal(ks[3], (H, Dh, D), dtype=jnp.float32) * scale, 'W_O': jax.random.normal(ks[4], (D, H * Dh), dtype=jnp.float32) * scale}
    _L0_attn_in = _L0_attn_setup()

    def _L0_ffn_setup():
        import jax, jax.numpy as jnp
        import numpy as np
        EPS = 1e-08

        def _quantize(w):
            gamma = jnp.mean(jnp.abs(w))
            return jnp.clip(jnp.round(w / (gamma + EPS)), -1.0, 1.0)

        def _bitlinear(x, w):
            return jnp.matmul(x, _quantize(w).T)
        key = jax.random.key(seed)
        k1, k2, k3, k4 = jax.random.split(key, 4)
        d, h = (256, 704)
        x = jax.random.normal(k1, (4, 256, d), dtype=jnp.float32)
        w1 = jax.random.normal(k2, (h, d), dtype=jnp.float32)
        w2 = jax.random.normal(k3, (h, d), dtype=jnp.float32)
        w3 = jax.random.normal(k4, (d, h), dtype=jnp.float32)
        return {'x': x, 'w1': w1, 'w2': w2, 'w3': w3}
    _L0_ffn_in = _L0_ffn_setup()
    _d = {'L0_attn_x': _L0_attn_in['x'], 'L0_attn_W_K': _L0_attn_in['W_K'], 'L0_attn_W_Q': _L0_attn_in['W_Q'], 'L0_attn_W_V': _L0_attn_in['W_V'], 'L0_attn_W_O': _L0_attn_in['W_O'], 'L0_ffn_w1': _L0_ffn_in['w1'], 'L0_ffn_w2': _L0_ffn_in['w2'], 'L0_ffn_w3': _L0_ffn_in['w3']}
    _x0 = _d['L0_attn_x']
    _d['L0_attn_x'] = jax.random.normal(jax.random.fold_in(jax.random.key(seed), 1), (4, 1024, 256), dtype=_x0.dtype)
    del _x0
    return _d

def reference(L0_attn_x, L0_attn_W_K, L0_attn_W_Q, L0_attn_W_V, L0_attn_W_O, L0_ffn_w1, L0_ffn_w2, L0_ffn_w3):

    def _L0_attn_ref(x, W_K, W_Q, W_V, W_O):
        import jax, jax.numpy as jnp
        import numpy as np
        b, pos, d_model = x.shape
        d_head = W_K.shape[1]
        k = jnp.einsum('ihd,bpd->biph', W_K, x)
        q = jnp.einsum('ihd,bpd->biph', W_Q, x)
        v = jnp.einsum('ihd,bpd->biph', W_V, x)
        scores = jnp.einsum('biph,biqh->biqp', k, q)
        mask = jnp.tril(jnp.ones((pos, pos), dtype=x.dtype))
        masked = scores * mask - jnp.float32(10000000000.0) * (1.0 - mask)
        attn = jax.nn.softmax(masked / jnp.sqrt(jnp.float32(d_head)), axis=-1)
        z = jnp.einsum('biqp,biph->biqh', attn, v)
        z_flat = jnp.transpose(z, (0, 2, 1, 3)).reshape(b, pos, -1)
        out = jnp.einsum('df,bqf->bqd', W_O, z_flat)
        return out

    def _L0_ffn_ref(x, w1, w2, w3):
        import jax, jax.numpy as jnp
        import numpy as np
        EPS = 1e-08

        def _quantize(w):
            gamma = jnp.mean(jnp.abs(w))
            return jnp.clip(jnp.round(w / (gamma + EPS)), -1.0, 1.0)

        def _bitlinear(x, w):
            return jnp.matmul(x, _quantize(w).T)
        x1 = _bitlinear(x, w1)
        x2 = _bitlinear(x, w2)
        hidden = jax.nn.sigmoid(x1) * x2
        return _bitlinear(hidden, w3)
    x = L0_attn_x
    x = x + _L0_attn_ref(_layernorm(x, axis=-1), L0_attn_W_K, L0_attn_W_Q, L0_attn_W_V, L0_attn_W_O)
    x = x + _L0_ffn_ref(_layernorm(x, axis=-1), L0_ffn_w1, L0_ffn_w2, L0_ffn_w3)
    return x

_drawn_inputs = setup_inputs


def setup_inputs(seed=0):
    import zlib

    import numpy as np

    out = dict(_drawn_inputs(seed))
    spreads = {}
    factors = {}
    for name, (base, spread) in spreads.items():
        noise = np.random.default_rng([zlib.crc32(name.encode()), seed]).standard_normal(out[name].shape)
        drawn = base * np.exp(spread * noise) if base else spread * noise
        out[name] = jnp.asarray(drawn.astype(out[name].dtype))
    for name, factor in factors.items():
        out[name] = (out[name] * factor).astype(out[name].dtype)
    return out
```

```python
import numpy as np
import concourse.bass as bass
from concourse import mybir
from contextlib import ExitStack

B, S, D, H, DH, F = 4, 1024, 256, 16, 128, 704
P = 128
DT = D // P
NB = S // P
CW = 512
CB = CW // P
HG = 2
NG = H // HG
GW = HG * DH
FT = -(-F // P)
FP = FT * P
ITS = B * NG
NCH = B * S // CW
EPS_LN = 1e-5
EPS_Q = 1e-8
SCALE = 1.0 / float(np.sqrt(np.float32(DH)))
MASKED = -1e10 * SCALE


UNITS = {"A0": ("A", 0), "A1": ("A", 1), "B0": ("B", 0), "B1": ("B", 1), "N0": ("A", 0), "P1": ("B", 1)}
S_FIRST = {"A1": 0, "B0": 4, "B1": 8, "N0": 12}
T_FIRST = {"A0": 0, "A1": 4, "B0": 12, "B1": 16}
TILES = {"A0": 4, "A1": 8, "B0": 4, "B1": 8}
ORDER = {"A0": 0, "A1": 1, "B0": 2, "B1": 3}
S_PER, T_PER, Z_PER, QK_PER, V_PER, PJ_PER, R_PER, W_PER, L_PER = 16, 24, 4, 8, 4, 12, 4, 4, 4
OB = 2

PASS = [
    ("T", "A0", 0), ("S", "A1", 0), ("T", "A0", 1), ("AV", "A0", 0), ("S", "A1", 1), ("T", "A0", 2), ("AV", "A0", 1),
    ("O", "P1", 0), ("S", "A1", 2), ("T", "A0", 3), ("AV", "A0", 2), ("O", "P1", 1), ("S", "A1", 3), ("AV", "A0", 3),
    ("V", 2), ("R", "A0"), ("QK", "B", 0), ("QK", "B", 1), ("T", "A1", 0), ("V", 3), ("T", "A1", 1), ("AV", "A1", 0),
    ("QK", "B", 2), ("T", "A1", 2), ("AV", "A1", 1), ("QK", "B", 3), ("T", "A1", 3), ("AV", "A1", 2), ("R", "A1"),
    ("O", "A0", 0), ("T", "A1", 4), ("AV", "A1", 3), ("S", "B0", 0), ("S", "B0", 1), ("T", "A1", 5), ("AV", "A1", 4),
    ("O", "A0", 1), ("S", "B0", 2), ("T", "A1", 6), ("AV", "A1", 5), ("S", "B0", 3), ("T", "A1", 7), ("AV", "A1", 6),
    ("T", "B0", 0), ("AV", "A1", 7), ("S", "B1", 0), ("T", "B0", 1), ("AV", "B0", 0), ("S", "B1", 1), ("R", "B0"),
    ("T", "B0", 2), ("AV", "B0", 1), ("O", "A1", 0), ("S", "B1", 2), ("T", "B0", 3), ("AV", "B0", 2), ("O", "A1", 1), ("L", 0),
    ("S", "B1", 3), ("L", 1), ("AV", "B0", 3), ("L", 2), ("L", 3),
    ("QK", "N", 0), ("QK", "N", 1), ("T", "B1", 0), ("O", "B0", 0), ("T", "B1", 1), ("AV", "B1", 0), ("R", "B1"),
    ("QK", "N", 2), ("T", "B1", 2), ("AV", "B1", 1), ("QK", "N", 3), ("T", "B1", 3), ("AV", "B1", 2),
    ("O", "B0", 1), ("T", "B1", 4), ("AV", "B1", 3), ("S", "N0", 0), ("S", "N0", 1), ("VN", 0), ("T", "B1", 5), ("AV", "B1", 4),
    ("S", "N0", 2), ("T", "B1", 6), ("AV", "B1", 5), ("VN", 1), ("S", "N0", 3), ("T", "B1", 7), ("AV", "B1", 6), ("AV", "B1", 7),
]
FOR_NEXT = [("QK", "N", 0), ("QK", "N", 1), ("QK", "N", 2), ("QK", "N", 3), ("S", "N0", 0), ("S", "N0", 1), ("VN", 0),
            ("S", "N0", 2), ("VN", 1), ("S", "N0", 3)]
FOR_LAST = [("O", "P1", 0), ("O", "P1", 1)]
S_PRE, QK_PRE, V_PRE = 4, 4, 2


def steps_of(kind):
    if kind == "before":
        return FOR_NEXT
    if kind == "after":
        return FOR_LAST
    return [s for s in PASS if not (
        (s[0] == "L" and kind != "turn") or (s in FOR_LAST and kind == "first") or (s in FOR_NEXT and kind == "last"))]


PJ_MADE = V_PRE
PJ_PRE = PJ_MADE - len(FOR_LAST)
PJ_SHIFT = {"before": PJ_PER - PJ_PRE, "first": len(FOR_LAST), "inner": 0, "turn": 0, "last": 0, "after": -PJ_MADE}


def pj_at(kind, it, step):
    made = [s for s in steps_of(kind) if s[0] in ("V", "VN", "O")]
    return PJ_PRE + PJ_PER * it + PJ_SHIFT[kind] + made.index(step)


def pj_start(kind, it):
    return PJ_PRE + PJ_PER * it + PJ_SHIFT[kind]


def build(nc, x, wqkv, wo, w1, w2, w3, out):
    f32, f32r = mybir.dt.float32, mybir.dt.float32r
    ALU, ACT, AX = mybir.AluOpType, mybir.ActivationFunctionType, mybir.AxisListType
    ds = bass.ds

    x_blocks = x.rearrange("b (n p) d -> p (b n) d", p=P)
    out_blocks = out.rearrange("b (n p) d -> p (b n) d", p=P)

    with ExitStack() as ctx:
        def sb(name, shape, dt=f32):
            return ctx.enter_context(nc.sbuf_tensor(name, shape, dt))

        def pb(name, shape):
            return ctx.enter_context(nc.psum_tensor(name, shape, f32))

        def sem(name):
            return ctx.enter_context(nc.semaphore(name))

        stream = sb("stream", [P, B * NB, D])
        xT = {n: sb(f"xT_{n}", [P, DT, S], f32r) for n in ("hi", "lo")}
        normed = sb("normed", [P, NB, D])
        QKW, VW = 2 * DT * DH, DT * GW
        raw_qkv = sb("raw_qkv", [P, 2 * QKW + VW])
        raw_o = sb("raw_o", [P, HG * D])
        w_qk = {(h, n): sb(f"w_qk_{h}_{n}", [P, 2, DT, DH], f32r) for h in "AB" for n in ("hi", "lo")}
        w_v = {n: sb(f"w_v_{n}", [P, DT, GW], f32r) for n in ("hi", "lo")}
        w_o = {n: sb(f"w_o_{n}", [P, HG, D], f32r) for n in ("hi", "lo")}
        qk = {n: sb(f"qk_{n}", [P, 2, S], f32r) for n in ("hi", "lo")}
        v = {n: sb(f"v_{n}", [P, NB, GW], f32r) for n in ("hi", "lo")}
        probs = [sb("probs_0", [P, CB, CW]), sb("probs_1", [P, CB, 2 * CW])]
        PT_RING = 3
        probsT = {n: sb(f"probsT_{n}", [P, PT_RING, CW], f32r) for n in ("hi", "lo")}
        z = {n: sb(f"z_{n}", [P, HG, S], f32r) for n in ("hi", "lo")}
        FW = FT * D
        raw_ff = sb("raw_ff", [P, 3, FW])
        w_up = [sb(f"w_up{i}", [P, DT, FP], f32r) for i in range(2)]
        w_down = sb("w_down", [P, FT, D], f32r)
        ident = sb("ident", [P, P])
        causal = sb("causal", [P, P])
        ones = sb("ones", [P, P])
        minus_half = sb("minus_half", [P, NB])
        neg_max = sb("neg_max", [P, S_PER])
        row_sum = sb("row_sum", [P, S_PER])
        row_rec = sb("row_rec", [P, S_PER])
        stats = sb("stats", [P, NB, 6])
        mean_var = sb("mean_var", [P, NB, 2])
        var_eps = sb("var_eps", [P, NB])
        rstd = sb("rstd", [P, NB])
        abs_sum = sb("abs_sum", [P, 3])
        limit = sb("limit", [P, 3])
        neg_limit = sb("neg_limit", [P, 3])

        scores = [pb(f"scores{i}", [P, 2 * CW]) for i in range(2)]
        turned = [pb(f"turned{i}", [P, CW]) for i in range(2)]
        z_bank = pb("z_bank", [P, CW])
        pj_bank = pb("pj_bank", [P, CW])

        x_in = [sem("x_in_first"), sem("x_in_rest")]
        const_made = sem("const_made")
        ff_in, ff_pad, ff_abs, ff_sum, ff_limit, ff_below, ff_above, ff_quant = (
            sem(n) for n in ("ff_in", "ff_pad", "ff_abs", "ff_sum", "ff_limit", "ff_below", "ff_above", "ff_quant"))
        qkv_in, wo_in, w_hi, w_split = (sem(n) for n in ("qkv_in", "wo_in", "w_hi", "w_split"))
        ln_stats, ln_mv, ln_eps, ln_rstd, ln_normed, ln_turned, ln_hi, ln_lo = (
            sem(n) for n in ("ln_stats", "ln_mv", "ln_eps", "ln_rstd", "ln_normed", "ln_turned", "ln_hi", "ln_lo"))
        pj_done, pj_out, values_hi = (sem(n) for n in ("pj_done", "pj_out", "values_hi"))
        qk_done, qk_hi, qk_out = (sem(n) for n in ("qk_done", "qk_hi", "qk_out"))
        s_done, s_masked, s_max, s_exp, s_rec = (sem(n) for n in ("s_done", "s_masked", "s_max", "s_exp", "s_rec"))
        t_done, t_hi, t_lo, av_done = (sem(n) for n in ("t_done", "t_hi", "t_lo", "av_done"))
        z_hi, z_lo = sem("z_hi"), sem("z_lo")
        up_done, sig_done, hid_done, hid_hi, hid_lo, down_done, down_added, out_done = (
            sem(n) for n in ("up_done", "sig_done", "hid_done", "hid_hi", "hid_lo", "down_done", "down_added", "out_done"))

        pool_held, dve_held = sem("pool_held"), sem("dve_held")

        block = ctx.enter_context(nc.Block())

        def wait(eng, s, n):
            if not (isinstance(n, int) and n <= 0):
                eng.wait_ge(s, n)

        def passes(eng, one):
            one("before", -1, -1, -1, -1)
            one("first", 0, 0, 0, 0)
            with eng.Fori(1, NG - 1) as g:
                one("inner", g, g, 0, 0)
            with eng.Fori(0, B - 1) as b:
                one("turn", b * NG + (NG - 1), NG - 1, b, b)
                with eng.Fori(0, NG - 1) as g:
                    it = b * NG + NG + g
                    one("inner", it, g, (it - 1) // NG, b + 1)
            one("last", ITS - 1, NG - 1, B - 1, B - 1)
            one("after", ITS, 0, B - 1, B)

        def s_at(it, unit, r):
            return S_PRE + it * S_PER + S_FIRST[unit] + r

        def qk_at(it, head, j):
            return QK_PRE + QK_PER * it + (4 if head == "N" else 0) + j

        def v_at(it, what, i):
            return V_PRE + V_PER * it + (2 + i if what == "VN" else i - 2)

        def qk_bank(j):
            return scores[j // 2][:, chunk_cols(j % 2)]

        def sum_col(unit, r):
            head, c = UNITS[unit]
            return "AB".index(head) * NB + c * CB + r

        def block_of(unit, r):
            qb = UNITS[unit][1] * CB + r
            return qb, (qb + 1) * P

        def tile_cols(unit, kb):
            return max(0, kb - UNITS[unit][1] * CB) * P

        def chunk_cols(c):
            return slice(c * CW, (c + 1) * CW)

        def hidden(n, f):
            if f < 4:
                return v[n][:, 2 * f:2 * f + 2, :].rearrange("p a b -> p (a b)")
            return z[n][:, f - 4, 0:CW]

        @block.sync
        def _(sp):
            def load_qkv(g):
                sp.dma_start(raw_qkv[:, :], wqkv[ds(g, 1)].rearrange("a p n -> p (a n)")).then_inc(qkv_in, 16)

            def load_o(g):
                sp.dma_start(raw_o[:, :], wo[ds(g, 1)].rearrange("a p n -> p (a n)")).then_inc(wo_in, 16)

            sp.dma_start(stream[:, 0:NB, :], x_blocks[:, 0:NB, :]).then_inc(x_in[0], 16)
            load_qkv(0)
            sp.wait_ge(ff_pad, 3)
            for i, w in enumerate((w1, w2)):
                dst = raw_ff[:, i, :].rearrange("p (t f) -> p t f", t=DT)[:, :, 0:F]
                sp.dma_start(dst, w.rearrange("(t p) f -> p t f", p=P)).then_inc(ff_in, 16)
            down = raw_ff[:, 2, :].rearrange("p (t d) -> p t d", t=FT)
            sp.dma_start(down[:, 0:FT - 1, :], w3[0:(FT - 1) * P, :].rearrange("(t p) d -> p t d", p=P)).then_inc(ff_in, 16)
            sp.dma_start(down[0:F - (FT - 1) * P, FT - 1, :], w3[(FT - 1) * P:F, :]).then_inc(ff_in, 16)
            for b in range(1, B):
                sp.dma_start(stream[:, b * NB:(b + 1) * NB, :], x_blocks[:, b * NB:(b + 1) * NB, :]).then_inc(x_in[1], 16)

            def one(kind, it, g, before, this):
                if kind in ("before", "after"):
                    return
                wait(sp, w_split, W_PER * it)
                load_o(g)
                if kind != "last":
                    sp.wait_ge(w_split, W_PER * it + 3)
                    load_qkv(0 if kind == "turn" else g + 1)

            passes(sp, one)

            with sp.Fori(0, NCH) as c:
                sp.wait_ge(down_added, 2 * c + 2)
                sp.dma_start(out_blocks[:, ds(c * CB, CB), :], stream[:, ds(c * CB, CB), :]).then_inc(out_done, 16)
            sp.wait_ge(out_done, 16 * NCH)

        @block.gpsimd
        def _(pool):
            gp = nc.gpsimd

            def hold(s, n):
                if not (isinstance(n, int) and n <= 0):
                    pool.wait_ge(s, n)
                    pool.sem_inc(pool_held, 1)

            gp.memset(raw_ff[:, 0, :], 0.0).then_inc(ff_pad, 1)
            gp.memset(raw_ff[:, 1, :], 0.0).then_inc(ff_pad, 1)
            gp.memset(raw_ff[:, 2, :], 0.0).then_inc(ff_pad, 1)
            gp.memset(ident[:, :], 0.0).then_inc(const_made, 1)
            gp.memset(causal[:, :], 0.0).then_inc(const_made, 1)
            gp.memset(minus_half[:, :], -0.5).then_inc(const_made, 1)
            gp.memset(ones[:, :], 1.0).then_inc(const_made, 1)
            pool.wait_ge(const_made, 4)
            gp.affine_select(out=ident[:, :], in_=ident[:, :], compare_op=ALU.not_equal, fill=1.0, base=0,
                             pattern=[[-1, P]], channel_multiplier=1).then_inc(const_made, 1)
            gp.affine_select(out=causal[:, :], in_=causal[:, :], compare_op=ALU.is_ge, fill=MASKED, base=0,
                             pattern=[[-1, P]], channel_multiplier=1).then_inc(const_made, 1)

            def split(raw, hi, lo, n):
                gp.tensor_copy(hi, raw).then_inc(w_hi, 1)
                hold(w_hi, n + 1)
                gp.tensor_tensor(lo, raw, hi.bitcast(f32), ALU.subtract).then_inc(w_split, 1)

            def flat(t):
                return t[:, :, :].rearrange("p a b -> p (a b)")

            def flat4(t):
                return t[:, :, :, :].rearrange("p a b c -> p (a b c)")

            def split_qk(head, n):
                at = 0 if head == "A" else QKW
                split(raw_qkv[:, at:at + QKW], flat4(w_qk[head, "hi"]), flat4(w_qk[head, "lo"]), n)

            def split_v(n):
                split(raw_qkv[:, 2 * QKW:], flat(w_v["hi"]), flat(w_v["lo"]), n)

            def norm_stats(n, count, blocks):
                hold(ln_mv, count + 1)
                hold(ln_normed, blocks)
                gp.tensor_scalar(var_eps[:, 0:n], mean_var[:, 0:n, 1], EPS_LN, None, ALU.add).then_inc(ln_eps, 1)
                hold(ln_eps, count + 1)
                gp.tensor_tensor(rstd[:, 0:n], var_eps[:, 0:n], minus_half[:, 0:n], ALU.pow).then_inc(ln_rstd, 1)

            pool.wait_ge(qkv_in, 16)
            split_qk("A", 0)
            split_v(1)
            split_qk("B", 2)
            norm_stats(NB, 0, 0)

            def quantise(k):
                i, part = divmod(k, 3)
                dst = (w_up[0], w_up[1], w_down)[i][:, :, :].rearrange("p a b -> p (a b)")
                below = dst.bitcast(f32)
                if part == 0:
                    if i == 0:
                        pool.wait_ge(ff_limit, 2)
                    gp.tensor_scalar(dst, raw_ff[:, i, :], neg_limit[:, i:i + 1], None, ALU.is_lt).then_inc(ff_below, 1)
                elif part == 1:
                    pool.wait_ge(ff_below, i + 1)
                    gp.tensor_scalar(raw_ff[:, i, :], raw_ff[:, i, :], limit[:, i:i + 1], None, ALU.is_gt).then_inc(ff_above, 1)
                else:
                    pool.wait_ge(ff_above, i + 1)
                    gp.tensor_tensor(dst, raw_ff[:, i, :], below, ALU.subtract).then_inc(ff_quant, 1)

            def one(kind, it, g, before, this):
                if kind in ("before", "after"):
                    return
                for step in steps_of(kind):
                    if step == ("R", "A0"):
                        hold(wo_in, 16 * (it + 1))
                        hold(pj_done, pj_at(kind, it, ("V", 2)))
                        split(raw_o[:, :], flat(w_o["hi"]), flat(w_o["lo"]), W_PER * it + 3)
                        if kind != "last":
                            hold(qkv_in, 16 * (it + 2))
                            hold(qk_done, qk_at(it, "B", 0))
                            split_qk("A", W_PER * (it + 1))
                            hold(pj_done, pj_at(kind, it, ("V", 3)) + 1)
                            split_v(W_PER * (it + 1) + 1)
                            if kind == "turn":
                                norm_stats(NB, before + 1, (before + 1) * NB)
                            hold(qk_done, qk_at(it, "B", 3) + 1)
                            split_qk("B", W_PER * (it + 1) + 2)
                        for k in range(9 if kind == "first" else 0):
                            quantise(k)

            passes(pool, one)

            with pool.Fori(0, NCH) as c:
                norm_stats(CB, B + c, NB * B + c * CB)

        @block.scalar
        def _(act):
            sc = nc.scalar

            def one(kind, it, g, before, this):
                for step in steps_of(kind):
                    what = step[0]
                    if what == "S":
                        unit, r = step[1:]
                        at = s_at(it, unit, r)
                        _, keys = block_of(unit, r)
                        if r == 0:
                            wait(act, t_done, T_PER * it + {"A1": 0, "B0": 4, "B1": 12, "N0": 16}[unit])
                        act.wait_ge(s_max, at + 1)
                        col = sum_col(unit, r)
                        sc.activation(probs[UNITS[unit][1]][:, r, 0:keys], scores[r % 2][:, 0:keys], ACT.Exp,
                                      bias=neg_max[:, col:col + 1], accum_out=row_sum[:, col:col + 1]).then_inc(s_exp, 1)
                    elif what == "T":
                        unit, kb = step[1:]
                        at = T_PER * it + T_FIRST[unit] + kb
                        c0 = tile_cols(unit, kb)
                        i = T_FIRST[unit] + kb
                        wait(act, av_done, at - PT_RING + 1)
                        act.wait_ge(t_done, at + 1)
                        sc.activation(probsT["hi"][:, i % PT_RING, c0:CW], turned[i % 2][:, c0:CW], ACT.Copy).then_inc(t_hi, 1)
                    elif what == "AV":
                        unit, kb = step[1:]
                        if kb == TILES[unit] - 1:
                            head, c = UNITS[unit]
                            wait(act, pj_done, (pj_start(kind, it) if kind != "first" else 0) + {"A0": 0, "A1": 0, "B0": 0, "B1": len(FOR_LAST)}[unit])
                            act.wait_ge(av_done, T_PER * it + T_FIRST[unit] + kb + 1)
                            sc.activation(z["hi"][:, "AB".index(head), chunk_cols(c)], z_bank[:, :], ACT.Copy).then_inc(z_hi, 1)
                    elif what in ("V", "VN"):
                        i = step[1]
                        wait(act, av_done, T_PER * it + (T_FIRST["B1"] + 2 * i + 2 if what == "VN" else 0))
                        act.wait_ge(pj_done, pj_at(kind, it, step) + 1)
                        dst = v["hi"][:, 2 * i:2 * i + 2, :].rearrange("p a b -> p (a b)")
                        sc.activation(dst, pj_bank[:, :], ACT.Copy).then_inc(values_hi, 1)
                    elif what == "QK":
                        head, j = step[1:]
                        wait(act, s_done, S_PRE + S_PER * it + (4 if head == "B" else 12))
                        act.wait_ge(qk_done, qk_at(it, head, j) + 1)
                        sc.activation(qk["hi"][:, j % 2, chunk_cols(j // 2)], qk_bank(j), ACT.Copy,
                                      scale=1.0 if j % 2 else SCALE).then_inc(qk_hi, 1)
                    elif what == "L":
                        if step[1] == 0:
                            act.wait_ge(pj_done, pj_at(kind, it, ("V", 3)) + 1)
                            act.wait_ge(qk_done, qk_at(it, "B", 3) + 1)
                        ln_part(step[1], before + 1)

            def ln_part(i, n):
                t, c = divmod(i, 2)
                act.wait_ge(ln_turned, L_PER * n + i + 1)
                sc.activation(xT["hi"][:, t, chunk_cols(c)], pj_bank[:, :], ACT.Copy).then_inc(ln_hi, 1)

            for i in range(L_PER):
                ln_part(i, 0)
            passes(act, one)

            def ln_chunk(c):
                for t in range(DT):
                    act.wait_ge(ln_turned, L_PER * B + DT * c + t + 1)
                    bank = (pj_bank, z_bank)[t]
                    dst = xT["hi"][:, t, ds((c % 2) * CW, CW)]
                    sc.activation(dst, bank[:, :], ACT.Copy).then_inc(ln_hi, 1)

            def chunk(c, last):
                for f in range(FT):
                    at = FT * c + f
                    act.wait_ge(up_done, at + 1)
                    wait(act, hid_done, at - 1)
                    sc.activation(probs[0][:, f % 2, :], scores[f % 2][:, 0:CW], ACT.Sigmoid).then_inc(sig_done, 1)
                    act.wait_ge(hid_done, at + 1)
                    sc.activation(hidden("hi", f), probs[0][:, 2 + f % 2, :], ACT.Copy).then_inc(hid_hi, 1)
                    if f == 2 and not last:
                        ln_chunk(c + 1)

            ln_chunk(0)
            chunk(0, False)
            with act.Fori(1, NCH - 1) as c:
                chunk(c, False)
            chunk(NCH - 1, True)

        @block.vector
        def _(dve):
            ve = nc.vector

            def lo_part(dst, src, hi, done, scale=None):
                if scale is None:
                    ve.tensor_tensor(dst, src, hi.bitcast(f32), ALU.subtract).then_inc(done, 1)
                else:
                    ve.scalar_tensor_tensor(out=dst, in0=src, scalar=scale, in1=hi.bitcast(f32),
                                            op0=ALU.mult, op1=ALU.subtract).then_inc(done, 1)

            def ln_stats_of(first_block, n, count, mv_count):
                for k in range(n):
                    ve.bn_stats(stats[:, k, :], stream[:, ds(first_block + k, 1), :].rearrange("p a b -> p (a b)")).then_inc(ln_stats, 1)
                dve.wait_ge(ln_stats, count + n)
                dve.sem_inc(dve_held, 1)
                for k in range(n):
                    last = ve.bn_aggr(mean_var[:, k, :], stats[:, k, :])
                last.then_inc(ln_mv, 1)

            def ln_apply(first_block, n, count, rstd_count):
                dve.wait_ge(ln_rstd, rstd_count)
                for k in range(n):
                    ve.tensor_scalar(normed[:, k, :], stream[:, ds(first_block + k, 1), :].rearrange("p a b -> p (a b)"),
                                     mean_var[:, k, 0:1], rstd[:, k:k + 1], ALU.subtract, ALU.mult).then_inc(ln_normed, 1)

            def ln_part(i, n):
                t, c = divmod(i, 2)
                dve.wait_ge(ln_hi, L_PER * n + i + 1)
                lo_part(xT["lo"][:, t, chunk_cols(c)], pj_bank[:, :], xT["hi"][:, t, chunk_cols(c)], ln_lo)

            def one(kind, it, g, before, this):
                for step in steps_of(kind):
                    what = step[0]
                    if what == "S":
                        unit, r = step[1:]
                        at = s_at(it, unit, r)
                        _, keys = block_of(unit, r)
                        tile = scores[r % 2]
                        diag = tile[:, keys - P:keys]
                        dve.wait_ge(s_done, at + 1)
                        ve.tensor_tensor(diag, diag, causal[:, :], ALU.add).then_inc(s_masked, 1)
                        dve.wait_ge(s_masked, at + 1)
                        col = sum_col(unit, r)
                        ve.tensor_reduce(neg_max[:, col:col + 1], tile[:, 0:keys], AX.X, ALU.max, negate=True).then_inc(s_max, 1)
                    elif what == "R":
                        unit = step[1]
                        col = sum_col(unit, 0)
                        dve.wait_ge(s_exp, S_PRE + S_PER * it + CB * ORDER[unit])
                        ve.reciprocal(row_rec[:, col:col + CB], row_sum[:, col:col + CB]).then_inc(s_rec, 1)
                    elif what == "T":
                        unit, kb = step[1:]
                        at = T_PER * it + T_FIRST[unit] + kb
                        c0 = tile_cols(unit, kb)
                        i = T_FIRST[unit] + kb
                        dve.wait_ge(t_hi, at + 1)
                        slot = i % PT_RING
                        lo_part(probsT["lo"][:, slot, c0:CW], turned[i % 2][:, c0:CW], probsT["hi"][:, slot, c0:CW], t_lo)
                    elif what == "AV":
                        unit, kb = step[1:]
                        if kb == TILES[unit] - 1:
                            head, c = UNITS[unit]
                            h = "AB".index(head)
                            dve.wait_ge(z_hi, Z_PER * it + ORDER[unit] + 1)
                            lo_part(z["lo"][:, h, chunk_cols(c)], z_bank[:, :], z["hi"][:, h, chunk_cols(c)], z_lo)
                    elif what in ("V", "VN"):
                        i = step[1]
                        dve.wait_ge(values_hi, v_at(it, what, i) + 1)
                        hi, lo = (v[n][:, 2 * i:2 * i + 2, :].rearrange("p a b -> p (a b)") for n in ("hi", "lo"))
                        lo_part(lo, pj_bank[:, :], hi, pj_out)
                        if kind == "turn" and step == ("V", 2):
                            dve.wait_ge(x_in[1], 16 * (B - 1))
                            ln_stats_of((before + 1) * NB, NB, (before + 1) * NB, 0)
                        if kind == "first" and i == 3:
                            dve.wait_ge(ff_in, 16 * 4)
                            ve.tensor_reduce(abs_sum[:, :], raw_ff[:, :, :], AX.X, ALU.add, apply_absolute_value=True).then_inc(ff_abs, 1)
                            dve.wait_ge(ff_sum, 1)
                            ve.tensor_scalar(limit[:, :], pj_bank[:, 0:3], 0.5 / (F * D), 0.5 * EPS_Q, ALU.mult, ALU.add).then_inc(ff_limit, 1)
                            ve.tensor_scalar(neg_limit[:, :], pj_bank[:, 0:3], -0.5 / (F * D), -0.5 * EPS_Q, ALU.mult, ALU.add).then_inc(ff_limit, 1)
                    elif what == "QK":
                        head, j = step[1:]
                        dve.wait_ge(qk_hi, qk_at(it, head, j) + 1)
                        cols = chunk_cols(j // 2)
                        lo_part(qk["lo"][:, j % 2, cols], qk_bank(j), qk["hi"][:, j % 2, cols], qk_out,
                                None if j % 2 else SCALE)
                        if kind == "turn" and step == ("QK", "B", 3):
                            ln_apply((before + 1) * NB, NB, 0, before + 2)
                    elif what == "O":
                        unit, i = step[1:]
                        dve.wait_ge(s_rec, R_PER * it + (0 if unit == "P1" else ORDER[unit] + 1))
                        dve.wait_ge(pj_done, pj_at(kind, it, step) + 1)
                        batch = before if unit == "P1" else this
                        for k in range(OB):
                            qb, _ = block_of(unit, OB * i + k)
                            col = sum_col(unit, OB * i + k)
                            dst = stream[:, ds(batch * NB + qb, 1), :].rearrange("p a b -> p (a b)")
                            last = ve.scalar_tensor_tensor(out=dst, in0=pj_bank[:, k * D:(k + 1) * D], scalar=row_rec[:, col:col + 1],
                                                           in1=dst, op0=ALU.mult, op1=ALU.add)
                        last.then_inc(pj_out, 1)
                    elif what == "L":
                        ln_part(step[1], before + 1)

            dve.wait_ge(x_in[0], 16)
            ln_stats_of(0, NB, 0, 0)
            ln_apply(0, NB, 0, 1)
            for i in range(L_PER):
                ln_part(i, 0)
            dve.wait_ge(const_made, 6)
            passes(dve, one)

            def ln_front(c):
                ln_stats_of(c * CB, CB, B * NB + CB * c, 0)
                ln_apply(c * CB, CB, 0, B + c + 1)

            def ln_chunk(c):
                for t in range(DT):
                    dve.wait_ge(ln_hi, L_PER * B + DT * c + t + 1)
                    bank = (pj_bank, z_bank)[t]
                    cols = ds((c % 2) * CW, CW)
                    lo_part(xT["lo"][:, t, cols], bank[:, :], xT["hi"][:, t, cols], ln_lo)

            def add_down(c):
                for i in range(2):
                    dve.wait_ge(down_done, c + 1)
                    dst = stream[:, ds(c * CB + 2 * i, 2), :].rearrange("p a b -> p (a b)")
                    ve.tensor_tensor(dst, turned[i][:, :], dst, ALU.add).then_inc(down_added, 1)

            def chunk(c, first, last):
                if not last:
                    ln_front(c + 1)
                for f in range(FT):
                    at = FT * c + f
                    dve.wait_ge(sig_done, at + 1)
                    wait(dve, hid_hi, at - 1)
                    ve.tensor_tensor(probs[0][:, 2 + f % 2, :], scores[f % 2][:, CW:2 * CW], probs[0][:, f % 2, :], ALU.mult).then_inc(hid_done, 1)
                    dve.wait_ge(hid_hi, at + 1)
                    lo_part(hidden("lo", f), probs[0][:, 2 + f % 2, :], hidden("hi", f), hid_lo)
                    if f == 1 and not first:
                        add_down(c - 1)
                    if f == 2 and not last:
                        ln_chunk(c + 1)

            dve.wait_ge(pj_out, pj_start("after", ITS) + len(FOR_LAST))
            ln_front(0)
            ln_chunk(0)
            chunk(0, True, False)
            with dve.Fori(1, NCH - 1) as c:
                chunk(c, False, False)
            chunk(NCH - 1, False, True)
            add_down(NCH - 1)

        @block.tensor
        def _(pe):
            te = nc.tensor

            def product(dst, pairs):
                todo = [(a(m), b(n)) for a, b in pairs for m, n in (("hi", "hi"), ("hi", "lo"), ("lo", "hi"))]
                for k, (a, b) in enumerate(todo):
                    last = te.matmul(dst, a, b, start=k == 0, stop=k == len(todo) - 1)
                return last

            def one(kind, it, g, before, this):
                for step in steps_of(kind):
                    what = step[0]
                    if what == "S":
                        unit, r = step[1:]
                        at = s_at(it, unit, r)
                        qb, keys = block_of(unit, r)
                        wait(pe, s_exp, at - 1)
                        if r == 0 and unit in ("B0", "N0"):
                            pe.wait_ge(qk_out, qk_at(it, "B" if unit == "B0" else "N", 3) + 1)
                        for c0 in range(0, keys, CW):
                            c1 = min(keys, c0 + CW)
                            last = product(scores[r % 2][:, c0:c1],
                                           [(lambda n: qk[n][:, 0, qb * P:(qb + 1) * P], lambda n: qk[n][:, 1, c0:c1])])
                        last.then_inc(s_done, 1)
                    elif what == "T":
                        unit, kb = step[1:]
                        i = T_FIRST[unit] + kb
                        at = T_PER * it + i
                        wait(pe, t_lo, at - 1)
                        if kb == 0:
                            pe.wait_ge(s_exp, S_PRE + S_PER * it + {"A0": 0, "A1": 4, "B0": 8, "B1": 12}[unit])
                        c0 = tile_cols(unit, kb)
                        for r in range(c0 // P, CB):
                            src = probs[UNITS[unit][1]][:, r, kb * P:(kb + 1) * P]
                            last = te.transpose(turned[i % 2][:, r * P:(r + 1) * P], src, ident[:, :])
                        last.then_inc(t_done, 1)
                    elif what == "AV":
                        unit, kb = step[1:]
                        head, c = UNITS[unit]
                        i = T_FIRST[unit] + kb
                        at = T_PER * it + i
                        if kb == 0:
                            wait(pe, z_lo, Z_PER * it + ORDER[unit])
                            if unit == "A0":
                                pe.wait_ge(pj_out, pj_start(kind, it))
                        if unit == "A1" and kb in (4, 6):
                            pe.wait_ge(pj_out, pj_at(kind, it, ("V", kb // 2)) + 1)
                        pe.wait_ge(t_hi, at + 1)
                        c0 = tile_cols(unit, kb)
                        h = "AB".index(head)
                        slot = i % PT_RING
                        n_tiles = TILES[unit]
                        for k, (m, n) in enumerate((("hi", "hi"), ("lo", "hi"), ("hi", "lo"))):
                            if k == 2:
                                pe.wait_ge(t_lo, at + 1)
                            last = te.matmul(z_bank[:, c0:CW], v[m][:, kb, h * DH:(h + 1) * DH], probsT[n][:, slot, c0:CW],
                                             start=kb == 0 and k == 0, stop=kb == n_tiles - 1 and k == 2)
                        last.then_inc(av_done, 1)
                    elif what in ("V", "VN"):
                        i = step[1]
                        wait(pe, pj_out, pj_at(kind, it, step))
                        if i % 2 == 0:
                            pe.wait_ge(w_split, W_PER * (it + (what == "VN")) + 2)
                        for k in range(2):
                            pb0 = 2 * i + k
                            last = product(pj_bank[:, k * GW:(k + 1) * GW],
                                           [(lambda n, t=t: xT[n][:, t, pb0 * P:(pb0 + 1) * P], lambda n, t=t: w_v[n][:, t, :])
                                            for t in range(DT)])
                        last.then_inc(pj_done, 1)
                        if kind == "first" and i == 3:
                            pe.wait_ge(ff_abs, 1)
                            te.matmul(pj_bank[:, 0:3], ones[:, :], abs_sum[:, :], start=True, stop=True).then_inc(ff_sum, 1)
                            pe.wait_ge(ff_limit, 2)
                    elif what == "QK":
                        head, j = step[1:]
                        wait(pe, s_exp, S_PRE + S_PER * it + (12 if head == "N" else 4) - 1 + j // 2)
                        if j == 0:
                            pe.wait_ge(w_split, W_PER * it + (3 if head == "B" else W_PER + 1))
                            if kind in ("before", "turn") and head == "N":
                                pe.wait_ge(ln_lo, L_PER * (before + 2))
                        w = "A" if head == "N" else "B"
                        cols = chunk_cols(j // 2)
                        product(qk_bank(j), [(lambda n, t=t: w_qk[w, n][:, j % 2, t, :], lambda n, t=t: xT[n][:, t, cols])
                                             for t in range(DT)]).then_inc(qk_done, 1)
                    elif what == "O":
                        unit, i = step[1:]
                        pe.wait_ge(pj_out, pj_at(kind, it, step))
                        if i == 0:
                            z_made = 0 if unit == "P1" else ORDER[unit] + 1
                            pe.wait_ge(z_lo, Z_PER * it + z_made)
                            pe.wait_ge(w_split, W_PER * (it if unit == "P1" else it + 1))
                        h = "AB".index(UNITS[unit][0])
                        for k in range(OB):
                            qb, _ = block_of(unit, OB * i + k)
                            last = product(pj_bank[:, k * D:(k + 1) * D],
                                           [(lambda n: z[n][:, h, qb * P:(qb + 1) * P], lambda n: w_o[n][:, h, :])])
                        last.then_inc(pj_done, 1)
                    elif what == "L":
                        i = step[1]
                        if i == 0:
                            pe.wait_ge(pj_out, pj_at(kind, it, ("O", "A1", 1)) + 1)
                        ln_part(i, before + 1)

            def ln_part(i, n):
                t, c = divmod(i, 2)
                wait(pe, ln_lo, L_PER * n + i)
                if i == 0:
                    pe.wait_ge(ln_normed, NB * (n + 1))
                for k in range(CB):
                    last = te.transpose(pj_bank[:, k * P:(k + 1) * P], normed[:, c * CB + k, t * P:(t + 1) * P], ident[:, :])
                last.then_inc(ln_turned, 1)

            pe.wait_ge(const_made, 6)
            for i in range(L_PER):
                ln_part(i, 0)
            passes(pe, one)

            def ln_chunk(c):
                for t in range(DT):
                    if t == 0:
                        pe.wait_ge(ln_normed, NB * B + CB * (c + 1))
                    pe.wait_ge(ln_lo, L_PER * B + DT * c)
                    for k in range(CB):
                        last = te.transpose((pj_bank, z_bank)[t][:, k * P:(k + 1) * P], normed[:, k, t * P:(t + 1) * P], ident[:, :])
                    last.then_inc(ln_turned, 1)

            def up(c, f):
                at = FT * c + f
                wait(pe, hid_done, at - 1)
                if f == 0:
                    pe.wait_ge(ln_lo, L_PER * B + DT * (c + 1))
                for u in range(2):
                    todo = [(t, n) for t in range(DT) for n in ("hi", "lo")]
                    for k, (t, n) in enumerate(todo):
                        last = te.matmul(scores[f % 2][:, u * CW:(u + 1) * CW], w_up[u][:, t, f * P:(f + 1) * P],
                                         xT[n][:, t, ds((c % 2) * CW, CW)], start=k == 0, stop=k == len(todo) - 1)
                last.then_inc(up_done, 1)

            def down(c, f):
                if f == 0:
                    wait(pe, down_added, 2 * c)
                pe.wait_ge(hid_lo, FT * c + f + 1)
                for r in range(CB):
                    bank = turned[r // 2]
                    for n in ("hi", "lo"):
                        last = te.matmul(bank[:, (r % 2) * D:(r % 2 + 1) * D], hidden(n, f)[:, r * P:(r + 1) * P], w_down[:, f, :],
                                         start=f == 0 and r % 2 == 0 and n == "hi", stop=f == FT - 1 and n == "lo",
                                         skip_group_check=True)
                if f == FT - 1:
                    last.then_inc(down_done, 1)

            LAG = 2

            def chunk(c, first, last):
                for f in range(FT):
                    up(c, f)
                    if f >= LAG:
                        down(c, f - LAG)
                    elif not first:
                        down(c - 1, FT - LAG + f)
                    if f == 2 and not last:
                        ln_chunk(c + 1)

            pe.wait_ge(ff_quant, 3)
            pe.wait_ge(pj_out, pj_start("after", ITS) + len(FOR_LAST))
            ln_chunk(0)
            chunk(0, True, False)
            with pe.Fori(1, NCH - 1) as c:
                chunk(c, False, False)
            chunk(NCH - 1, False, True)
            for f in range(FT - LAG, FT):
                down(NCH - 1, f)


def kernel(L0_attn_x, L0_attn_W_K, L0_attn_W_Q, L0_attn_W_V, L0_attn_W_O, L0_ffn_w1, L0_ffn_w2, L0_ffn_w3):
    import concourse.bacc as bacc
    from concourse.bass_utils import run_bass_kernel_spmd

    def by_head(w):
        return np.asarray(w).reshape(NG, HG, DH, DT, P).transpose(0, 4, 1, 3, 2)

    q, k, v = by_head(L0_attn_W_Q), by_head(L0_attn_W_K), by_head(L0_attn_W_V)
    qk = np.stack([q, k], axis=3).reshape(NG, P, HG * 2 * DT * DH)
    v = v.transpose(0, 1, 3, 2, 4).reshape(NG, P, DT * GW)
    o = np.asarray(L0_attn_W_O).reshape(D, NG, HG, DH).transpose(1, 3, 2, 0).reshape(NG, P, HG * D)
    arrays = {
        "x": np.ascontiguousarray(L0_attn_x),
        "wqkv": np.ascontiguousarray(np.concatenate([qk, v], axis=2)),
        "wo": np.ascontiguousarray(o),
        "w1": np.ascontiguousarray(np.asarray(L0_ffn_w1).T),
        "w2": np.ascontiguousarray(np.asarray(L0_ffn_w2).T),
        "w3": np.ascontiguousarray(np.asarray(L0_ffn_w3).T),
    }
    nc = bacc.Bacc("TRN2", target_bir_lowering=False, num_devices=1)
    args = [nc.dram_tensor(n, a.shape, mybir.dt.from_np(a.dtype), kind="ExternalInput").ap() for n, a in arrays.items()]
    out = nc.dram_tensor("out", (B, S, D), mybir.dt.float32, kind="ExternalOutput").ap()
    build(nc, *args, out)
    return run_bass_kernel_spmd(nc, [arrays], core_ids=[0]).results[0]["out"]
```

```python
import numpy as np
import concourse.bass as bass
from concourse import mybir
from contextlib import ExitStack

B, S, D, H, DH, F = 4, 1024, 256, 16, 128, 704
P = 128
DT = D // P
NB = S // P
CW = 512
CB = CW // P
HG = 2
NG = H // HG
GW = HG * DH
FT = -(-F // P)
FP = FT * P
ITS = B * NG
NCH = B * S // CW
EPS_LN = 1e-5
EPS_Q = 1e-8
SCALE = 1.0 / float(np.sqrt(np.float32(DH)))
MASKED = -1e10 * SCALE


UNITS = {"A0": ("A", 0), "A1": ("A", 1), "B0": ("B", 0), "B1": ("B", 1), "N0": ("A", 0), "P1": ("B", 1)}
S_FIRST = {"A1": 0, "B0": 4, "B1": 8, "N0": 12}
T_FIRST = {"A0": 0, "A1": 4, "B0": 12, "B1": 16, "P1": -8}
TILES = {"A0": 4, "A1": 8, "B0": 4, "B1": 8, "P1": 8}
ORDER = {"A0": 0, "A1": 1, "B0": 2, "B1": 3, "P1": -1}
S_PER, T_PER, Z_PER, QK_PER, V_PER, PJ_PER, R_PER, W_PER, L_PER = 16, 24, 4, 8, 4, 12, 4, 4, 4
OB = 2

PASS = [
    ("AV", "P1", 7), ("S", "A1", 0), ("AE", "P1"), ("S", "A1", 1), ("V", 2), ("S", "A1", 2), ("T", "A0", 0), ("R", "A0"),
    ("T", "A0", 1), ("S", "A1", 3), ("AV", "A0", 0), ("O", "P1", 0), ("AV", "A0", 1), ("T", "A0", 2), ("T", "A0", 3),
    ("QK", "B", 0), ("QK", "B", 1), ("AV", "A0", 2), ("AV", "A0", 3), ("T", "A1", 0), ("O", "P1", 1), ("T", "A1", 1),
    ("QK", "B", 2), ("AE", "A0"), ("QK", "B", 3), ("T", "A1", 2), ("V", 3), ("AV", "A1", 0), ("S", "B0", 0),
    ("T", "A1", 3), ("AV", "A1", 1), ("AV", "A1", 2), ("S", "B0", 1), ("T", "A1", 4), ("S", "B0", 2), ("T", "A1", 5),
    ("AV", "A1", 3), ("AV", "A1", 4), ("S", "B0", 3), ("T", "A1", 6), ("O", "A0", 0), ("AV", "A1", 5), ("T", "A1", 7),
    ("S", "B1", 0), ("T", "B0", 0), ("AV", "A1", 6), ("AV", "A1", 7), ("O", "A0", 1), ("T", "B0", 1), ("AE", "A1"),
    ("L", 0), ("S", "B1", 1), ("L", 1), ("T", "B0", 2), ("S", "B1", 2), ("L", 2), ("AV", "B0", 0), ("R", "A1"),
    ("AV", "B0", 1), ("T", "B0", 3), ("AV", "B0", 2), ("L", 3), ("O", "A1", 0), ("S", "B1", 3), ("AV", "B0", 3),
    ("AE", "B0"), ("QK", "N", 0), ("QK", "N", 1), ("O", "A1", 1), ("T", "B1", 0), ("QK", "N", 2), ("T", "B1", 1),
    ("AV", "B1", 0), ("QK", "N", 3), ("R", "B0"), ("T", "B1", 2), ("O", "B0", 0), ("R", "B1"), ("T", "B1", 3),
    ("AV", "B1", 1), ("S", "N0", 0), ("AV", "B1", 2), ("S", "N0", 1), ("T", "B1", 4), ("AV", "B1", 3), ("VN", 0),
    ("S", "N0", 2), ("AV", "B1", 4), ("T", "B1", 5), ("T", "B1", 6), ("VN", 1), ("AV", "B1", 5), ("S", "N0", 3),
    ("AV", "B1", 6), ("T", "B1", 7), ("O", "B0", 1),
]
FOR_NEXT = [("QK", "N", 0), ("QK", "N", 1), ("QK", "N", 2), ("QK", "N", 3), ("VN", 0), ("S", "N0", 0), ("S", "N0", 1),
            ("S", "N0", 2), ("S", "N0", 3), ("VN", 1)]
FOR_LAST = [("AV", "P1", 7), ("AE", "P1"), ("O", "P1", 0), ("O", "P1", 1)]
S_PRE, QK_PRE, V_PRE = 4, 4, 2


def with_late_exponentials(steps):
    out, held = [], None
    for s in steps:
        if s[0] == "S":
            if held:
                out.append(held)
            held = s
        elif held and s[0] in ("T", "AE", "V", "VN", "QK"):
            out += [held, s] if s[0] == "T" and UNITS[s[1]] == UNITS[held[1]] else [s, held]
            held = None
        else:
            out.append(s)
    return out + ([held] if held else [])


def steps_of(kind):
    if kind == "before":
        return FOR_NEXT
    if kind == "after":
        return FOR_LAST
    return [s for s in PASS if not (
        (s[0] == "L" and kind != "turn") or (s in FOR_LAST and kind == "first") or (s in FOR_NEXT and kind == "last"))]


PJ_MADE, O_PREV = V_PRE, 2
PJ_PRE = PJ_MADE - O_PREV
PJ_SHIFT = {"before": PJ_PER - PJ_PRE, "first": O_PREV, "inner": 0, "turn": 0, "last": 0, "after": -PJ_MADE}


def pj_at(kind, it, step):
    steps = steps_of(kind)
    made = sum(s[0] in ("V", "VN", "O") for s in steps[:steps.index(step)])
    return PJ_PRE + PJ_PER * it + PJ_SHIFT[kind] + made


def pj_start(kind, it):
    return PJ_PRE + PJ_PER * it + PJ_SHIFT[kind]


def build(nc, x, wqkv, wo, w1, w2, w3, out):
    f32, f32r = mybir.dt.float32, mybir.dt.float32r
    ALU, ACT, AX = mybir.AluOpType, mybir.ActivationFunctionType, mybir.AxisListType
    ds = bass.ds

    x_blocks = x.rearrange("b (n p) d -> p (b n) d", p=P)
    out_blocks = out.rearrange("b (n p) d -> p (b n) d", p=P)

    with ExitStack() as ctx:
        def sb(name, shape, dt=f32):
            return ctx.enter_context(nc.sbuf_tensor(name, shape, dt))

        def pb(name, shape):
            return ctx.enter_context(nc.psum_tensor(name, shape, f32))

        def sem(name):
            return ctx.enter_context(nc.semaphore(name))

        stream = sb("stream", [P, B * NB, D])
        xT = {n: sb(f"xT_{n}", [P, DT, S], f32r) for n in ("hi", "lo")}
        normed = sb("normed", [P, NB, D])
        QKW, VW = 2 * DT * DH, DT * GW
        raw_qkv = sb("raw_qkv", [P, 2 * QKW + VW])
        raw_o = sb("raw_o", [P, HG * D])
        w_qk = {(h, n): sb(f"w_qk_{h}_{n}", [P, 2, DT, DH], f32r) for h in "AB" for n in ("hi", "lo")}
        w_v = {n: sb(f"w_v_{n}", [P, DT, GW], f32r) for n in ("hi", "lo")}
        w_o = {n: sb(f"w_o_{n}", [P, HG, D], f32r) for n in ("hi", "lo")}
        qk = {n: sb(f"qk_{n}", [P, 2, S], f32r) for n in ("hi", "lo")}
        v = {n: sb(f"v_{n}", [P, NB, GW], f32r) for n in ("hi", "lo")}
        probs = [sb("probs_0", [P, CB, CW]), sb("probs_1", [P, CB, 2 * CW])]
        PT_RING = 3
        probsT = {n: sb(f"probsT_{n}", [P, PT_RING, CW], f32r) for n in ("hi", "lo")}
        z = {n: sb(f"z_{n}", [P, HG, S], f32r) for n in ("hi", "lo")}
        FW = FT * D
        raw_ff = sb("raw_ff", [P, 3, FW])
        w_up = [sb(f"w_up{i}", [P, DT, FP], f32r) for i in range(2)]
        w_down = sb("w_down", [P, FT, D], f32r)
        ident = sb("ident", [P, P])
        causal = sb("causal", [P, P])
        ones = sb("ones", [P, P])
        minus_half = sb("minus_half", [P, NB])
        neg_max = sb("neg_max", [P, S_PER])
        row_sum = sb("row_sum", [P, S_PER])
        row_rec = sb("row_rec", [P, S_PER])
        stats = sb("stats", [P, NB, 6])
        mean_var = sb("mean_var", [P, NB, 2])
        var_eps = sb("var_eps", [P, NB])
        rstd = sb("rstd", [P, NB])
        abs_sum = sb("abs_sum", [P, 3])
        limit = sb("limit", [P, 3])
        neg_limit = sb("neg_limit", [P, 3])

        scores = [pb(f"scores{i}", [P, 2 * CW]) for i in range(2)]
        turned = [pb(f"turned{i}", [P, CW]) for i in range(2)]
        z_bank = pb("z_bank", [P, CW])
        pj_bank = pb("pj_bank", [P, CW])

        x_in = [sem("x_in_first"), sem("x_in_rest")]
        const_made = sem("const_made")
        ff_in, ff_pad, ff_abs, ff_sum, ff_limit, ff_below, ff_above, ff_quant = (
            sem(n) for n in ("ff_in", "ff_pad", "ff_abs", "ff_sum", "ff_limit", "ff_below", "ff_above", "ff_quant"))
        qkv_in, wo_in, w_hi, w_split = (sem(n) for n in ("qkv_in", "wo_in", "w_hi", "w_split"))
        ln_stats, ln_mv, ln_eps, ln_rstd, ln_normed, ln_turned, ln_hi, ln_lo = (
            sem(n) for n in ("ln_stats", "ln_mv", "ln_eps", "ln_rstd", "ln_normed", "ln_turned", "ln_hi", "ln_lo"))
        pj_done, pj_out, values_hi = (sem(n) for n in ("pj_done", "pj_out", "values_hi"))
        qk_done, qk_hi, qk_out = (sem(n) for n in ("qk_done", "qk_hi", "qk_out"))
        s_done, s_masked, s_max, s_exp, s_rec = (sem(n) for n in ("s_done", "s_masked", "s_max", "s_exp", "s_rec"))
        t_done, t_hi, t_lo, av_done = (sem(n) for n in ("t_done", "t_hi", "t_lo", "av_done"))
        z_hi, z_lo = sem("z_hi"), sem("z_lo")
        up_done, sig_done, hid_done, hid_hi, hid_lo, down_done, down_added, out_done = (
            sem(n) for n in ("up_done", "sig_done", "hid_done", "hid_hi", "hid_lo", "down_done", "down_added", "out_done"))

        pool_held, dve_held = sem("pool_held"), sem("dve_held")

        block = ctx.enter_context(nc.Block())

        def wait(eng, s, n):
            if not (isinstance(n, int) and n <= 0):
                eng.wait_ge(s, n)

        def passes(eng, one):
            one("before", -1, -1, -1, -1)
            one("first", 0, 0, 0, 0)
            with eng.Fori(1, NG - 1) as g:
                one("inner", g, g, 0, 0)
            with eng.Fori(0, B - 1) as b:
                one("turn", b * NG + (NG - 1), NG - 1, b, b)
                with eng.Fori(0, NG - 1) as g:
                    it = b * NG + NG + g
                    one("inner", it, g, (it - 1) // NG, b + 1)
            one("last", ITS - 1, NG - 1, B - 1, B - 1)
            one("after", ITS, 0, B - 1, B)

        def s_at(it, unit, r):
            return S_PRE + it * S_PER + S_FIRST[unit] + r

        def qk_at(it, head, j):
            return QK_PRE + QK_PER * it + (4 if head == "N" else 0) + j

        def v_at(it, what, i):
            return V_PRE + V_PER * it + (2 + i if what == "VN" else i - 2)

        def qk_bank(j):
            return scores[j // 2][:, chunk_cols(j % 2)]

        def sum_col(unit, r):
            head, c = UNITS[unit]
            return "AB".index(head) * NB + c * CB + r

        def block_of(unit, r):
            qb = UNITS[unit][1] * CB + r
            return qb, (qb + 1) * P

        def tile_cols(unit, kb):
            return max(0, kb - UNITS[unit][1] * CB) * P

        def chunk_cols(c):
            return slice(c * CW, (c + 1) * CW)

        def hidden(n, f):
            if f < 4:
                return v[n][:, 2 * f:2 * f + 2, :].rearrange("p a b -> p (a b)")
            return z[n][:, f - 4, 0:CW]

        @block.sync
        def _(sp):
            def load_qkv(g):
                sp.dma_start(raw_qkv[:, :], wqkv[ds(g, 1)].rearrange("a p n -> p (a n)")).then_inc(qkv_in, 16)

            def load_o(g):
                sp.dma_start(raw_o[:, :], wo[ds(g, 1)].rearrange("a p n -> p (a n)")).then_inc(wo_in, 16)

            sp.dma_start(stream[:, 0:NB, :], x_blocks[:, 0:NB, :]).then_inc(x_in[0], 16)
            load_qkv(0)
            sp.wait_ge(ff_pad, 3)
            for i, w in enumerate((w1, w2)):
                dst = raw_ff[:, i, :].rearrange("p (t f) -> p t f", t=DT)[:, :, 0:F]
                sp.dma_start(dst, w.rearrange("(t p) f -> p t f", p=P)).then_inc(ff_in, 16)
            down = raw_ff[:, 2, :].rearrange("p (t d) -> p t d", t=FT)
            sp.dma_start(down[:, 0:FT - 1, :], w3[0:(FT - 1) * P, :].rearrange("(t p) d -> p t d", p=P)).then_inc(ff_in, 16)
            sp.dma_start(down[0:F - (FT - 1) * P, FT - 1, :], w3[(FT - 1) * P:F, :]).then_inc(ff_in, 16)
            for b in range(1, B):
                sp.dma_start(stream[:, b * NB:(b + 1) * NB, :], x_blocks[:, b * NB:(b + 1) * NB, :]).then_inc(x_in[1], 16)

            def one(kind, it, g, before, this):
                if kind in ("before", "after"):
                    return
                wait(sp, w_split, W_PER * it)
                load_o(g)
                if kind != "last":
                    sp.wait_ge(w_split, W_PER * it + 3)
                    load_qkv(0 if kind == "turn" else g + 1)

            passes(sp, one)

            with sp.Fori(0, NCH) as c:
                sp.wait_ge(down_added, 2 * c + 2)
                sp.dma_start(out_blocks[:, ds(c * CB, CB), :], stream[:, ds(c * CB, CB), :]).then_inc(out_done, 16)
            sp.wait_ge(out_done, 16 * NCH)

        @block.gpsimd
        def _(pool):
            gp = nc.gpsimd

            def hold(s, n):
                if not (isinstance(n, int) and n <= 0):
                    pool.wait_ge(s, n)
                    pool.sem_inc(pool_held, 1)

            gp.memset(raw_ff[:, 0, :], 0.0).then_inc(ff_pad, 1)
            gp.memset(raw_ff[:, 1, :], 0.0).then_inc(ff_pad, 1)
            gp.memset(raw_ff[:, 2, :], 0.0).then_inc(ff_pad, 1)
            gp.memset(ident[:, :], 0.0).then_inc(const_made, 1)
            gp.memset(causal[:, :], 0.0).then_inc(const_made, 1)
            gp.memset(minus_half[:, :], -0.5).then_inc(const_made, 1)
            gp.memset(ones[:, :], 1.0).then_inc(const_made, 1)
            pool.wait_ge(const_made, 4)
            gp.affine_select(out=ident[:, :], in_=ident[:, :], compare_op=ALU.not_equal, fill=1.0, base=0,
                             pattern=[[-1, P]], channel_multiplier=1).then_inc(const_made, 1)
            gp.affine_select(out=causal[:, :], in_=causal[:, :], compare_op=ALU.is_ge, fill=MASKED, base=0,
                             pattern=[[-1, P]], channel_multiplier=1).then_inc(const_made, 1)

            def split(raw, hi, lo, n):
                gp.tensor_copy(hi, raw).then_inc(w_hi, 1)
                hold(w_hi, n + 1)
                gp.tensor_tensor(lo, raw, hi.bitcast(f32), ALU.subtract).then_inc(w_split, 1)

            def flat(t):
                return t[:, :, :].rearrange("p a b -> p (a b)")

            def flat4(t):
                return t[:, :, :, :].rearrange("p a b c -> p (a b c)")

            def split_qk(head, n):
                at = 0 if head == "A" else QKW
                split(raw_qkv[:, at:at + QKW], flat4(w_qk[head, "hi"]), flat4(w_qk[head, "lo"]), n)

            def split_v(n):
                split(raw_qkv[:, 2 * QKW:], flat(w_v["hi"]), flat(w_v["lo"]), n)

            def norm_stats(n, count, blocks):
                hold(ln_mv, count + 1)
                hold(ln_normed, blocks)
                gp.tensor_scalar(var_eps[:, 0:n], mean_var[:, 0:n, 1], EPS_LN, None, ALU.add).then_inc(ln_eps, 1)
                hold(ln_eps, count + 1)
                gp.tensor_tensor(rstd[:, 0:n], var_eps[:, 0:n], minus_half[:, 0:n], ALU.pow).then_inc(ln_rstd, 1)

            pool.wait_ge(qkv_in, 16)
            split_qk("A", 0)
            split_v(1)
            split_qk("B", 2)
            norm_stats(NB, 0, 0)

            def quantise(k):
                i, part = divmod(k, 3)
                dst = (w_up[0], w_up[1], w_down)[i][:, :, :].rearrange("p a b -> p (a b)")
                below = dst.bitcast(f32)
                if part == 0:
                    if i == 0:
                        pool.wait_ge(ff_limit, 2)
                    gp.tensor_scalar(dst, raw_ff[:, i, :], neg_limit[:, i:i + 1], None, ALU.is_lt).then_inc(ff_below, 1)
                elif part == 1:
                    pool.wait_ge(ff_below, i + 1)
                    gp.tensor_scalar(raw_ff[:, i, :], raw_ff[:, i, :], limit[:, i:i + 1], None, ALU.is_gt).then_inc(ff_above, 1)
                else:
                    pool.wait_ge(ff_above, i + 1)
                    gp.tensor_tensor(dst, raw_ff[:, i, :], below, ALU.subtract).then_inc(ff_quant, 1)

            def one(kind, it, g, before, this):
                if kind in ("before", "after"):
                    return
                for step in steps_of(kind):
                    if step == ("R", "A0"):
                        hold(wo_in, 16 * (it + 1))
                        if kind != "first":
                            hold(pj_done, pj_at(kind, it, ("O", "P1", 1)) + 1)
                        split(raw_o[:, :], flat(w_o["hi"]), flat(w_o["lo"]), W_PER * it + 3)
                        if kind != "last":
                            hold(qkv_in, 16 * (it + 2))
                            hold(qk_done, qk_at(it, "B", 0))
                            split_qk("A", W_PER * (it + 1))
                            hold(pj_done, pj_at(kind, it, ("V", 3)) + 1)
                            split_v(W_PER * (it + 1) + 1)
                            if kind == "turn":
                                norm_stats(NB, before + 1, (before + 1) * NB)
                            hold(qk_done, qk_at(it, "B", 3) + 1)
                            split_qk("B", W_PER * (it + 1) + 2)
                        for k in range(9 if kind == "first" else 0):
                            quantise(k)

            passes(pool, one)

            with pool.Fori(0, NCH) as c:
                norm_stats(CB, B + c, NB * B + c * CB)

        @block.scalar
        def _(act):
            sc = nc.scalar

            def one(kind, it, g, before, this):
                for step in with_late_exponentials(steps_of(kind)):
                    what = step[0]
                    if what == "S":
                        unit, r = step[1:]
                        at = s_at(it, unit, r)
                        _, keys = block_of(unit, r)
                        if r == 0:
                            wait(act, t_done, T_PER * it + {"A1": 0, "B0": 4, "B1": 12, "N0": 16}[unit])
                        act.wait_ge(s_max, at + 1)
                        col = sum_col(unit, r)
                        sc.activation(probs[UNITS[unit][1]][:, r, 0:keys], scores[r % 2][:, 0:keys], ACT.Exp,
                                      bias=neg_max[:, col:col + 1], accum_out=row_sum[:, col:col + 1]).then_inc(s_exp, 1)
                    elif what == "T":
                        unit, kb = step[1:]
                        at = T_PER * it + T_FIRST[unit] + kb
                        c0 = tile_cols(unit, kb)
                        i = T_FIRST[unit] + kb
                        wait(act, av_done, at - PT_RING + 1)
                        act.wait_ge(t_done, at + 1)
                        sc.activation(probsT["hi"][:, i % PT_RING, c0:CW], turned[i % 2][:, c0:CW], ACT.Copy).then_inc(t_hi, 1)
                    elif what == "AE":
                        unit = step[1]
                        head, c = UNITS[unit]
                        if kind != "first":
                            act.wait_ge(pj_done, pj_start(kind, it) + (O_PREV if unit == "B1" else 0))
                        act.wait_ge(av_done, T_PER * it + T_FIRST[unit] + TILES[unit])
                        sc.activation(z["hi"][:, "AB".index(head), chunk_cols(c)], z_bank[:, :], ACT.Copy).then_inc(z_hi, 1)
                    elif what in ("V", "VN"):
                        i = step[1]
                        wait(act, av_done, T_PER * it + (T_FIRST["B1"] + 2 * i + 2 if what == "VN" else 0))
                        act.wait_ge(pj_done, pj_at(kind, it, step) + 1)
                        dst = v["hi"][:, 2 * i:2 * i + 2, :].rearrange("p a b -> p (a b)")
                        sc.activation(dst, pj_bank[:, :], ACT.Copy).then_inc(values_hi, 1)
                    elif what == "QK":
                        head, j = step[1:]
                        wait(act, s_done, S_PRE + S_PER * it + (4 if head == "B" else 12))
                        act.wait_ge(qk_done, qk_at(it, head, j) + 1)
                        sc.activation(qk["hi"][:, j % 2, chunk_cols(j // 2)], qk_bank(j), ACT.Copy,
                                      scale=1.0 if j % 2 else SCALE).then_inc(qk_hi, 1)
                    elif what == "L":
                        if step[1] == 0:
                            act.wait_ge(pj_done, pj_at(kind, it, ("V", 3)) + 1)
                            act.wait_ge(qk_done, qk_at(it, "B", 3) + 1)
                        ln_part(step[1], before + 1)

            def ln_part(i, n):
                t, c = divmod(i, 2)
                act.wait_ge(ln_turned, L_PER * n + i + 1)
                sc.activation(xT["hi"][:, t, chunk_cols(c)], pj_bank[:, :], ACT.Copy).then_inc(ln_hi, 1)

            for i in range(L_PER):
                ln_part(i, 0)
            passes(act, one)

            def ln_chunk(c):
                for t in range(DT):
                    act.wait_ge(ln_turned, L_PER * B + DT * c + t + 1)
                    bank = (pj_bank, z_bank)[t]
                    dst = xT["hi"][:, t, ds((c % 2) * CW, CW)]
                    sc.activation(dst, bank[:, :], ACT.Copy).then_inc(ln_hi, 1)

            def chunk(c, last):
                for f in range(FT):
                    at = FT * c + f
                    act.wait_ge(up_done, at + 1)
                    wait(act, hid_done, at - 1)
                    sc.activation(probs[0][:, f % 2, :], scores[f % 2][:, 0:CW], ACT.Sigmoid).then_inc(sig_done, 1)
                    act.wait_ge(hid_done, at + 1)
                    sc.activation(hidden("hi", f), probs[0][:, 2 + f % 2, :], ACT.Copy).then_inc(hid_hi, 1)
                    if f == 2 and not last:
                        ln_chunk(c + 1)

            ln_chunk(0)
            chunk(0, False)
            with act.Fori(1, NCH - 1) as c:
                chunk(c, False)
            chunk(NCH - 1, True)

        @block.vector
        def _(dve):
            ve = nc.vector

            def lo_part(dst, src, hi, done, scale=None):
                if scale is None:
                    ve.tensor_tensor(dst, src, hi.bitcast(f32), ALU.subtract).then_inc(done, 1)
                else:
                    ve.scalar_tensor_tensor(out=dst, in0=src, scalar=scale, in1=hi.bitcast(f32),
                                            op0=ALU.mult, op1=ALU.subtract).then_inc(done, 1)

            def ln_block_stats(first_block, k):
                ve.bn_stats(stats[:, k, :], stream[:, ds(first_block + k, 1), :].rearrange("p a b -> p (a b)")).then_inc(ln_stats, 1)

            def ln_mean_var(n, count):
                dve.wait_ge(ln_stats, count + n)
                dve.sem_inc(dve_held, 1)
                for k in range(n):
                    last = ve.bn_aggr(mean_var[:, k, :], stats[:, k, :])
                last.then_inc(ln_mv, 1)

            def ln_stats_of(first_block, n, count):
                for k in range(n):
                    ln_block_stats(first_block, k)
                ln_mean_var(n, count)

            def ln_apply(first_block, blocks, rstd_count):
                dve.wait_ge(ln_rstd, rstd_count)
                for k in blocks:
                    ve.tensor_scalar(normed[:, k, :], stream[:, ds(first_block + k, 1), :].rearrange("p a b -> p (a b)"),
                                     mean_var[:, k, 0:1], rstd[:, k:k + 1], ALU.subtract, ALU.mult).then_inc(ln_normed, 1)

            def ln_part(i, n):
                t, c = divmod(i, 2)
                dve.wait_ge(ln_hi, L_PER * n + i + 1)
                lo_part(xT["lo"][:, t, chunk_cols(c)], pj_bank[:, :], xT["hi"][:, t, chunk_cols(c)], ln_lo)

            def one(kind, it, g, before, this):
                for step in steps_of(kind):
                    what = step[0]
                    if what == "S":
                        unit, r = step[1:]
                        at = s_at(it, unit, r)
                        _, keys = block_of(unit, r)
                        tile = scores[r % 2]
                        diag = tile[:, keys - P:keys]
                        dve.wait_ge(s_done, at + 1)
                        ve.tensor_tensor(diag, diag, causal[:, :], ALU.add).then_inc(s_masked, 1)
                        dve.wait_ge(s_masked, at + 1)
                        col = sum_col(unit, r)
                        ve.tensor_reduce(neg_max[:, col:col + 1], tile[:, 0:keys], AX.X, ALU.max, negate=True).then_inc(s_max, 1)
                    elif what == "R":
                        unit = step[1]
                        col = sum_col(unit, 0)
                        dve.wait_ge(s_exp, S_PRE + S_PER * it + CB * ORDER[unit])
                        ve.reciprocal(row_rec[:, col:col + CB], row_sum[:, col:col + CB]).then_inc(s_rec, 1)
                    elif what == "T":
                        unit, kb = step[1:]
                        at = T_PER * it + T_FIRST[unit] + kb
                        c0 = tile_cols(unit, kb)
                        i = T_FIRST[unit] + kb
                        dve.wait_ge(t_hi, at + 1)
                        slot = i % PT_RING
                        lo_part(probsT["lo"][:, slot, c0:CW], turned[i % 2][:, c0:CW], probsT["hi"][:, slot, c0:CW], t_lo)
                        if kind == "turn" and i < NB:
                            if i == 0:
                                dve.wait_ge(x_in[1], 16 * (B - 1))
                            ln_block_stats((before + 1) * NB, i)
                            if i == NB - 1:
                                ln_mean_var(NB, (before + 1) * NB)
                        if kind == "turn" and NB < i <= NB + 4:
                            k = 2 * (i - NB - 1)
                            ln_apply((before + 1) * NB, (k, k + 1), before + 2)
                    elif what == "AE":
                        unit = step[1]
                        head, c = UNITS[unit]
                        h = "AB".index(head)
                        dve.wait_ge(z_hi, Z_PER * it + ORDER[unit] + 1)
                        lo_part(z["lo"][:, h, chunk_cols(c)], z_bank[:, :], z["hi"][:, h, chunk_cols(c)], z_lo)
                    elif what in ("V", "VN"):
                        i = step[1]
                        dve.wait_ge(values_hi, v_at(it, what, i) + 1)
                        hi, lo = (v[n][:, 2 * i:2 * i + 2, :].rearrange("p a b -> p (a b)") for n in ("hi", "lo"))
                        lo_part(lo, pj_bank[:, :], hi, pj_out)
                        if kind == "first" and i == 3:
                            dve.wait_ge(ff_in, 16 * 4)
                            ve.tensor_reduce(abs_sum[:, :], raw_ff[:, :, :], AX.X, ALU.add, apply_absolute_value=True).then_inc(ff_abs, 1)
                            dve.wait_ge(ff_sum, 1)
                            ve.tensor_scalar(limit[:, :], pj_bank[:, 0:3], 0.5 / (F * D), 0.5 * EPS_Q, ALU.mult, ALU.add).then_inc(ff_limit, 1)
                            ve.tensor_scalar(neg_limit[:, :], pj_bank[:, 0:3], -0.5 / (F * D), -0.5 * EPS_Q, ALU.mult, ALU.add).then_inc(ff_limit, 1)
                    elif what == "QK":
                        head, j = step[1:]
                        dve.wait_ge(qk_hi, qk_at(it, head, j) + 1)
                        cols = chunk_cols(j // 2)
                        lo_part(qk["lo"][:, j % 2, cols], qk_bank(j), qk["hi"][:, j % 2, cols], qk_out,
                                None if j % 2 else SCALE)
                    elif what == "O":
                        unit, i = step[1:]
                        dve.wait_ge(s_rec, R_PER * it + (0 if unit == "P1" else ORDER[unit] + 1))
                        dve.wait_ge(pj_done, pj_at(kind, it, step) + 1)
                        batch = before if unit == "P1" else this
                        for k in range(OB):
                            qb, _ = block_of(unit, OB * i + k)
                            col = sum_col(unit, OB * i + k)
                            dst = stream[:, ds(batch * NB + qb, 1), :].rearrange("p a b -> p (a b)")
                            last = ve.scalar_tensor_tensor(out=dst, in0=pj_bank[:, k * D:(k + 1) * D], scalar=row_rec[:, col:col + 1],
                                                           in1=dst, op0=ALU.mult, op1=ALU.add)
                        last.then_inc(pj_out, 1)
                    elif what == "L":
                        ln_part(step[1], before + 1)

            dve.wait_ge(x_in[0], 16)
            ln_stats_of(0, NB, 0)
            ln_apply(0, range(NB), 1)
            for i in range(L_PER):
                ln_part(i, 0)
            dve.wait_ge(const_made, 6)
            passes(dve, one)

            def ln_front(c):
                ln_stats_of(c * CB, CB, B * NB + CB * c)
                ln_apply(c * CB, range(CB), B + c + 1)

            def ln_chunk(c):
                for t in range(DT):
                    dve.wait_ge(ln_hi, L_PER * B + DT * c + t + 1)
                    bank = (pj_bank, z_bank)[t]
                    cols = ds((c % 2) * CW, CW)
                    lo_part(xT["lo"][:, t, cols], bank[:, :], xT["hi"][:, t, cols], ln_lo)

            def add_down(c):
                for i in range(2):
                    dve.wait_ge(down_done, c + 1)
                    dst = stream[:, ds(c * CB + 2 * i, 2), :].rearrange("p a b -> p (a b)")
                    ve.tensor_tensor(dst, turned[i][:, :], dst, ALU.add).then_inc(down_added, 1)

            def chunk(c, first, last):
                if not last:
                    ln_front(c + 1)
                for f in range(FT):
                    at = FT * c + f
                    dve.wait_ge(sig_done, at + 1)
                    wait(dve, hid_hi, at - 1)
                    ve.tensor_tensor(probs[0][:, 2 + f % 2, :], scores[f % 2][:, CW:2 * CW], probs[0][:, f % 2, :], ALU.mult).then_inc(hid_done, 1)
                    dve.wait_ge(hid_hi, at + 1)
                    lo_part(hidden("lo", f), probs[0][:, 2 + f % 2, :], hidden("hi", f), hid_lo)
                    if f == 1 and not first:
                        add_down(c - 1)
                    if f == 2 and not last:
                        ln_chunk(c + 1)

            dve.wait_ge(pj_out, pj_start("after", ITS) + O_PREV)
            ln_front(0)
            ln_chunk(0)
            chunk(0, True, False)
            with dve.Fori(1, NCH - 1) as c:
                chunk(c, False, False)
            chunk(NCH - 1, False, True)
            add_down(NCH - 1)

        @block.tensor
        def _(pe):
            te = nc.tensor

            def product(dst, pairs):
                todo = [(a(m), b(n)) for a, b in pairs for m, n in (("hi", "hi"), ("hi", "lo"), ("lo", "hi"))]
                for k, (a, b) in enumerate(todo):
                    last = te.matmul(dst, a, b, start=k == 0, stop=k == len(todo) - 1)
                return last

            def av_lo(it, unit, kb):
                i = T_FIRST[unit] + kb
                c0 = tile_cols(unit, kb)
                h = "AB".index(UNITS[unit][0])
                pe.wait_ge(t_lo, T_PER * it + i + 1)
                te.matmul(z_bank[:, c0:CW], v["hi"][:, kb, h * DH:(h + 1) * DH], probsT["lo"][:, i % PT_RING, c0:CW],
                          start=False, stop=kb == TILES[unit] - 1).then_inc(av_done, 1)

            def pj_bank_free(kind, it, before, step):
                wait(pe, pj_out, pj_at(kind, it, step))
                steps = steps_of(kind)
                users = [s for s in steps[:steps.index(step)] if s[0] in ("V", "VN", "O", "L")]
                if users and users[-1][0] == "L" and step[0] != "L":
                    pe.wait_ge(ln_lo, L_PER * (before + 2))

            def one(kind, it, g, before, this):
                for step in steps_of(kind):
                    what = step[0]
                    if what == "S":
                        unit, r = step[1:]
                        at = s_at(it, unit, r)
                        qb, keys = block_of(unit, r)
                        wait(pe, s_exp, at - 1)
                        if r == 0 and unit in ("B0", "N0"):
                            pe.wait_ge(qk_out, qk_at(it, "B" if unit == "B0" else "N", 3) + 1)
                        for c0 in range(0, keys, CW):
                            c1 = min(keys, c0 + CW)
                            last = product(scores[r % 2][:, c0:c1],
                                           [(lambda n: qk[n][:, 0, qb * P:(qb + 1) * P], lambda n: qk[n][:, 1, c0:c1])])
                        last.then_inc(s_done, 1)
                    elif what == "T":
                        unit, kb = step[1:]
                        i = T_FIRST[unit] + kb
                        at = T_PER * it + i
                        wait(pe, t_lo, at - 1)
                        if kb == 0:
                            pe.wait_ge(s_exp, S_PRE + S_PER * it + {"A0": 0, "A1": 4, "B0": 8, "B1": 12}[unit])
                        c0 = tile_cols(unit, kb)
                        for r in range(c0 // P, CB):
                            src = probs[UNITS[unit][1]][:, r, kb * P:(kb + 1) * P]
                            last = te.transpose(turned[i % 2][:, r * P:(r + 1) * P], src, ident[:, :])
                        last.then_inc(t_done, 1)
                    elif what == "AV":
                        unit, kb = step[1:]
                        head, c = UNITS[unit]
                        i = T_FIRST[unit] + kb
                        at = T_PER * it + i
                        if kb == 0:
                            wait(pe, z_lo, Z_PER * it + ORDER[unit])
                            if unit == "A0":
                                pe.wait_ge(pj_out, pj_start(kind, it))
                        if unit == "A1" and kb in (4, 6):
                            pe.wait_ge(pj_out, pj_at(kind, it, ("V", kb // 2)) + 1)
                        if kb > 0:
                            av_lo(it, unit, kb - 1)
                        pe.wait_ge(t_hi, at + 1)
                        c0 = tile_cols(unit, kb)
                        h = "AB".index(head)
                        for m in ("hi", "lo"):
                            te.matmul(z_bank[:, c0:CW], v[m][:, kb, h * DH:(h + 1) * DH], probsT["hi"][:, i % PT_RING, c0:CW],
                                      start=kb == 0 and m == "hi", stop=False)
                    elif what == "AE":
                        av_lo(it, step[1], TILES[step[1]] - 1)
                    elif what in ("V", "VN"):
                        i = step[1]
                        pj_bank_free(kind, it, before, step)
                        if i % 2 == 0:
                            pe.wait_ge(w_split, W_PER * (it + (what == "VN")) + 2)
                        for k in range(2):
                            pb0 = 2 * i + k
                            last = product(pj_bank[:, k * GW:(k + 1) * GW],
                                           [(lambda n, t=t: xT[n][:, t, pb0 * P:(pb0 + 1) * P], lambda n, t=t: w_v[n][:, t, :])
                                            for t in range(DT)])
                        last.then_inc(pj_done, 1)
                        if kind == "first" and i == 3:
                            pe.wait_ge(ff_abs, 1)
                            te.matmul(pj_bank[:, 0:3], ones[:, :], abs_sum[:, :], start=True, stop=True).then_inc(ff_sum, 1)
                            pe.wait_ge(ff_limit, 2)
                    elif what == "QK":
                        head, j = step[1:]
                        wait(pe, s_exp, S_PRE + S_PER * it + (12 if head == "N" else 4) - 1 + j // 2)
                        if j == 0:
                            pe.wait_ge(w_split, W_PER * it + (3 if head == "B" else W_PER + 1))
                            if kind in ("before", "turn") and head == "N":
                                pe.wait_ge(ln_lo, L_PER * (before + 2))
                        w = "A" if head == "N" else "B"
                        cols = chunk_cols(j // 2)
                        product(qk_bank(j), [(lambda n, t=t: w_qk[w, n][:, j % 2, t, :], lambda n, t=t: xT[n][:, t, cols])
                                             for t in range(DT)]).then_inc(qk_done, 1)
                    elif what == "O":
                        unit, i = step[1:]
                        pj_bank_free(kind, it, before, step)
                        if i == 0:
                            z_made = 0 if unit == "P1" else ORDER[unit] + 1
                            pe.wait_ge(z_lo, Z_PER * it + z_made)
                            pe.wait_ge(w_split, W_PER * (it if unit == "P1" else it + 1))
                        h = "AB".index(UNITS[unit][0])
                        for k in range(OB):
                            qb, _ = block_of(unit, OB * i + k)
                            last = product(pj_bank[:, k * D:(k + 1) * D],
                                           [(lambda n: z[n][:, h, qb * P:(qb + 1) * P], lambda n: w_o[n][:, h, :])])
                        last.then_inc(pj_done, 1)
                    elif what == "L":
                        i = step[1]
                        if i == 0:
                            pj_bank_free(kind, it, before, step)
                        ln_part(i, before + 1)

            def ln_part(i, n):
                t, c = divmod(i, 2)
                wait(pe, ln_lo, L_PER * n + i)
                if i == 0:
                    pe.wait_ge(ln_normed, NB * (n + 1))
                for k in range(CB):
                    last = te.transpose(pj_bank[:, k * P:(k + 1) * P], normed[:, c * CB + k, t * P:(t + 1) * P], ident[:, :])
                last.then_inc(ln_turned, 1)

            pe.wait_ge(const_made, 6)
            for i in range(L_PER):
                ln_part(i, 0)
            passes(pe, one)

            def ln_chunk(c):
                for t in range(DT):
                    if t == 0:
                        pe.wait_ge(ln_normed, NB * B + CB * (c + 1))
                    pe.wait_ge(ln_lo, L_PER * B + DT * c)
                    for k in range(CB):
                        last = te.transpose((pj_bank, z_bank)[t][:, k * P:(k + 1) * P], normed[:, k, t * P:(t + 1) * P], ident[:, :])
                    last.then_inc(ln_turned, 1)

            def up(c, f):
                at = FT * c + f
                wait(pe, hid_done, at - 1)
                if f == 0:
                    pe.wait_ge(ln_lo, L_PER * B + DT * (c + 1))
                for u in range(2):
                    todo = [(t, n) for t in range(DT) for n in ("hi", "lo")]
                    for k, (t, n) in enumerate(todo):
                        last = te.matmul(scores[f % 2][:, u * CW:(u + 1) * CW], w_up[u][:, t, f * P:(f + 1) * P],
                                         xT[n][:, t, ds((c % 2) * CW, CW)], start=k == 0, stop=k == len(todo) - 1)
                last.then_inc(up_done, 1)

            def down(c, f):
                if f == 0:
                    wait(pe, down_added, 2 * c)
                pe.wait_ge(hid_lo, FT * c + f + 1)
                for r in range(CB):
                    bank = turned[r // 2]
                    for n in ("hi", "lo"):
                        last = te.matmul(bank[:, (r % 2) * D:(r % 2 + 1) * D], hidden(n, f)[:, r * P:(r + 1) * P], w_down[:, f, :],
                                         start=f == 0 and r % 2 == 0 and n == "hi", stop=f == FT - 1 and n == "lo",
                                         skip_group_check=True)
                if f == FT - 1:
                    last.then_inc(down_done, 1)

            LAG = 2

            def chunk(c, first, last):
                for f in range(FT):
                    up(c, f)
                    if f >= LAG:
                        down(c, f - LAG)
                    elif not first:
                        down(c - 1, FT - LAG + f)
                    if f == 2 and not last:
                        ln_chunk(c + 1)

            pe.wait_ge(ff_quant, 3)
            pe.wait_ge(pj_out, pj_start("after", ITS) + O_PREV)
            ln_chunk(0)
            chunk(0, True, False)
            with pe.Fori(1, NCH - 1) as c:
                chunk(c, False, False)
            chunk(NCH - 1, False, True)
            for f in range(FT - LAG, FT):
                down(NCH - 1, f)


def kernel(L0_attn_x, L0_attn_W_K, L0_attn_W_Q, L0_attn_W_V, L0_attn_W_O, L0_ffn_w1, L0_ffn_w2, L0_ffn_w3):
    import concourse.bacc as bacc
    from concourse.bass_utils import run_bass_kernel_spmd

    def by_head(w):
        return np.asarray(w).reshape(NG, HG, DH, DT, P).transpose(0, 4, 1, 3, 2)

    q, k, v = by_head(L0_attn_W_Q), by_head(L0_attn_W_K), by_head(L0_attn_W_V)
    qk = np.stack([q, k], axis=3).reshape(NG, P, HG * 2 * DT * DH)
    v = v.transpose(0, 1, 3, 2, 4).reshape(NG, P, DT * GW)
    o = np.asarray(L0_attn_W_O).reshape(D, NG, HG, DH).transpose(1, 3, 2, 0).reshape(NG, P, HG * D)
    arrays = {
        "x": np.ascontiguousarray(L0_attn_x),
        "wqkv": np.ascontiguousarray(np.concatenate([qk, v], axis=2)),
        "wo": np.ascontiguousarray(o),
        "w1": np.ascontiguousarray(np.asarray(L0_ffn_w1).T),
        "w2": np.ascontiguousarray(np.asarray(L0_ffn_w2).T),
        "w3": np.ascontiguousarray(np.asarray(L0_ffn_w3).T),
    }
    nc = bacc.Bacc("TRN2", target_bir_lowering=False, num_devices=1)
    args = [nc.dram_tensor(n, a.shape, mybir.dt.from_np(a.dtype), kind="ExternalInput").ap() for n, a in arrays.items()]
    out = nc.dram_tensor("out", (B, S, D), mybir.dt.float32, kind="ExternalOutput").ap()
    build(nc, *args, out)
    return run_bass_kernel_spmd(nc, [arrays], core_ids=[0]).results[0]["out"]
```

```python
import numpy as np
import concourse.bass as bass
from concourse import mybir
from contextlib import ExitStack

B, S, D, H, DH, F = 4, 1024, 256, 16, 128, 704
P = 128
DT = D // P
NB = S // P
CW = 512
CB = CW // P
HG = 2
NG = H // HG
GW = HG * DH
FT = -(-F // P)
FP = FT * P
ITS = B * NG
NCH = B * S // CW
EPS_LN = 1e-5
EPS_Q = 1e-8
SCALE = 1.0 / float(np.sqrt(np.float32(DH)))
MASKED = -1e10 * SCALE


UNITS = {"A0": ("A", 0), "A1": ("A", 1), "B0": ("B", 0), "B1": ("B", 1), "N0": ("A", 0), "P1": ("B", 1)}
S_FIRST = {"A1": 0, "B0": 4, "B1": 8, "N0": 12}
T_FIRST = {"A0": 0, "A1": 4, "B0": 12, "B1": 16, "P1": -8}
TILES = {"A0": 4, "A1": 8, "B0": 4, "B1": 8, "P1": 8}
ORDER = {"A0": 0, "A1": 1, "B0": 2, "B1": 3, "P1": -1}
S_PER, T_PER, Z_PER, QK_PER, V_PER, PJ_PER, R_PER, W_PER, L_PER = 16, 24, 4, 8, 4, 12, 4, 4, 4
OB = 2

PASS = [
    ("S", "A1", 0), ("AV", "P1", 7), ("AE", "P1"), ("S", "A1", 1), ("R", "A0"), ("V", 2), ("S", "A1", 2), ("T", "A0", 0),
    ("S", "A1", 3), ("T", "A0", 1), ("O", "P1", 0), ("AV", "A0", 0), ("T", "A0", 2), ("QK", "B", 0), ("AV", "A0", 1),
    ("T", "A0", 3), ("QK", "B", 1), ("AV", "A0", 2), ("O", "P1", 1), ("T", "A1", 0), ("AV", "A0", 3), ("AE", "A0"),
    ("QK", "B", 2), ("QK", "B", 3), ("T", "A1", 1), ("T", "A1", 2), ("V", 3), ("AV", "A1", 0), ("S", "B0", 0),
    ("T", "A1", 3), ("AV", "A1", 1), ("S", "B0", 1), ("T", "A1", 4), ("AV", "A1", 2), ("AV", "A1", 3), ("S", "B0", 2),
    ("L", 0), ("T", "A1", 5), ("AV", "A1", 4), ("S", "B0", 3), ("T", "A1", 6), ("O", "A0", 0), ("AV", "A1", 5),
    ("T", "A1", 7), ("S", "B1", 0), ("L", 2), ("T", "B0", 0), ("R", "B0"), ("AV", "A1", 6), ("S", "B1", 1), ("L", 1),
    ("AV", "A1", 7), ("AE", "A1"), ("S", "B1", 2), ("O", "A0", 1), ("R", "A1"), ("T", "B0", 1), ("AV", "B0", 0),
    ("S", "B1", 3), ("T", "B0", 2), ("AV", "B0", 1), ("O", "A1", 0), ("AV", "B0", 2), ("T", "B0", 3), ("QK", "N", 0),
    ("L", 3), ("QK", "N", 1), ("T", "B1", 0), ("AV", "B0", 3), ("T", "B1", 1), ("AE", "B0"), ("QK", "N", 2),
    ("O", "A1", 1), ("QK", "N", 3), ("T", "B1", 2), ("AV", "B1", 0), ("AV", "B1", 1), ("O", "B0", 0), ("T", "B1", 3),
    ("AV", "B1", 2), ("S", "N0", 0), ("T", "B1", 4), ("VN", 0), ("T", "B1", 5), ("AV", "B1", 3), ("S", "N0", 1),
    ("T", "B1", 6), ("AV", "B1", 4), ("S", "N0", 2), ("R", "B1"), ("VN", 1), ("S", "N0", 3), ("AV", "B1", 5),
    ("AV", "B1", 6), ("T", "B1", 7), ("O", "B0", 1),
]
BEFORE = [("L", 0), ("L", 2), ("L", 1), ("L", 3), ("QK", "N", 0), ("QK", "N", 1), ("QK", "N", 2), ("QK", "N", 3), ("VN", 0),
          ("S", "N0", 0), ("S", "N0", 1), ("VN", 1), ("S", "N0", 2), ("S", "N0", 3)]
FOR_NEXT = [s for s in BEFORE if s[0] != "L"]
FOR_LAST = [("AV", "P1", 7), ("AE", "P1"), ("O", "P1", 0), ("O", "P1", 1)]
S_PRE, QK_PRE, V_PRE = 4, 4, 2

FF_SUM_AT = [("T", "A0", 3), ("AE", "A0"), ("QK", "B", 3)]
FF_LIMIT_AT, FF_LIMIT_AFTER, FF_LIMIT_BEFORE = ("S", "B0", 2), ("V", 3), ("O", "A0", 0)


def with_late_exponentials(steps):
    out, held = [], None
    for s in steps:
        if s[0] == "S":
            if held:
                out.append(held)
            held = s
        elif held and s[0] in ("T", "AE", "V", "VN", "QK"):
            out += [held, s] if s[0] == "T" and UNITS[s[1]] == UNITS[held[1]] else [s, held]
            held = None
        else:
            out.append(s)
    return out + ([held] if held else [])


def steps_of(kind):
    if kind == "before":
        return BEFORE
    if kind == "after":
        return FOR_LAST
    return [s for s in PASS if not (
        (s[0] == "L" and kind not in ("turn", "last")) or (s in FOR_LAST and kind == "first") or (s in FOR_NEXT and kind == "last"))]


PJ_MADE, O_PREV = V_PRE, 2
PJ_PRE = PJ_MADE - O_PREV
PJ_SHIFT = {"before": PJ_PER - PJ_PRE, "first": O_PREV, "inner": 0, "turn": 0, "last": 0, "after": -PJ_MADE}


def pj_at(kind, it, step):
    steps = steps_of(kind)
    made = sum(s[0] in ("V", "VN", "O") for s in steps[:steps.index(step)])
    return PJ_PRE + PJ_PER * it + PJ_SHIFT[kind] + made


def pj_start(kind, it):
    return PJ_PRE + PJ_PER * it + PJ_SHIFT[kind]


def build(nc, x, wqkv, wo, w1, w2, w3, out):
    f32, f32r = mybir.dt.float32, mybir.dt.float32r
    ALU, ACT, AX = mybir.AluOpType, mybir.ActivationFunctionType, mybir.AxisListType
    ds = bass.ds

    x_blocks = x.rearrange("b (n p) d -> p (b n) d", p=P)
    out_blocks = out.rearrange("b (n p) d -> p (b n) d", p=P)

    with ExitStack() as ctx:
        def sb(name, shape, dt=f32):
            return ctx.enter_context(nc.sbuf_tensor(name, shape, dt))

        def pb(name, shape):
            return ctx.enter_context(nc.psum_tensor(name, shape, f32))

        def sem(name):
            return ctx.enter_context(nc.semaphore(name))

        stream = sb("stream", [P, B * NB, D])
        xT = {n: sb(f"xT_{n}", [P, DT, S], f32r) for n in ("hi", "lo")}
        normed = sb("normed", [P, NB, D])
        QKW, VW = 2 * DT * DH, DT * GW
        raw_qkv = sb("raw_qkv", [P, 2 * QKW + VW])
        raw_o = sb("raw_o", [P, HG * D])
        w_qk = {(h, n): sb(f"w_qk_{h}_{n}", [P, 2, DT, DH], f32r) for h in "AB" for n in ("hi", "lo")}
        w_v = {n: sb(f"w_v_{n}", [P, DT, GW], f32r) for n in ("hi", "lo")}
        w_o = {n: sb(f"w_o_{n}", [P, HG, D], f32r) for n in ("hi", "lo")}
        qk = {n: sb(f"qk_{n}", [P, 2, S], f32r) for n in ("hi", "lo")}
        v = {n: sb(f"v_{n}", [P, NB, GW], f32r) for n in ("hi", "lo")}
        probs = [sb("probs_0", [P, CB, CW]), sb("probs_1", [P, CB, 2 * CW])]
        PT_RING = 3
        probsT = {n: sb(f"probsT_{n}", [P, PT_RING, CW], f32r) for n in ("hi", "lo")}
        z = {n: sb(f"z_{n}", [P, HG, S], f32r) for n in ("hi", "lo")}
        FW = FT * D
        raw_ff = sb("raw_ff", [P, 3, FW])
        w_up = [sb(f"w_up{i}", [P, DT, FP], f32r) for i in range(2)]
        w_down = sb("w_down", [P, FT, D], f32r)
        ident = sb("ident", [P, P])
        causal = sb("causal", [P, P])
        ones = sb("ones", [P, P])
        minus_half = sb("minus_half", [P, NB])
        neg_max = sb("neg_max", [P, S_PER])
        row_sum = sb("row_sum", [P, S_PER])
        row_rec = sb("row_rec", [P, S_PER])
        stats = sb("stats", [P, NB, 6])
        mean_var = sb("mean_var", [P, NB, 2])
        var_eps = sb("var_eps", [P, NB])
        rstd = sb("rstd", [P, NB])
        abs_sum = sb("abs_sum", [P, 3])
        limit = sb("limit", [P, 3])
        neg_limit = sb("neg_limit", [P, 3])

        scores = [pb(f"scores{i}", [P, 2 * CW]) for i in range(2)]
        turned = [pb(f"turned{i}", [P, CW]) for i in range(2)]
        z_bank = pb("z_bank", [P, CW])
        pj_bank = pb("pj_bank", [P, CW])

        x_in = [sem("x_in_half_0"), sem("x_in_half_1"), sem("x_in_rest")]
        const_made = sem("const_made")
        ff_in, ff_pad, ff_abs, ff_sum, ff_limit, ff_below, ff_above, ff_quant = (
            sem(n) for n in ("ff_in", "ff_pad", "ff_abs", "ff_sum", "ff_limit", "ff_below", "ff_above", "ff_quant"))
        qkv_in, wo_in, w_hi, w_split = (sem(n) for n in ("qkv_in", "wo_in", "w_hi", "w_split"))
        ln_stats, ln_mv, ln_eps, ln_rstd, ln_normed, ln_turned, ln_hi, ln_lo = (
            sem(n) for n in ("ln_stats", "ln_mv", "ln_eps", "ln_rstd", "ln_normed", "ln_turned", "ln_hi", "ln_lo"))
        pj_done, pj_out, values_hi = (sem(n) for n in ("pj_done", "pj_out", "values_hi"))
        qk_done, qk_hi, qk_out = (sem(n) for n in ("qk_done", "qk_hi", "qk_out"))
        s_done, s_masked, s_max, s_exp, s_rec = (sem(n) for n in ("s_done", "s_masked", "s_max", "s_exp", "s_rec"))
        t_done, t_hi, t_lo, av_done = (sem(n) for n in ("t_done", "t_hi", "t_lo", "av_done"))
        z_hi, z_lo = sem("z_hi"), sem("z_lo")
        up_done, sig_done, hid_done, hid_hi, hid_lo, down_done, down_added, out_done = (
            sem(n) for n in ("up_done", "sig_done", "hid_done", "hid_hi", "hid_lo", "down_done", "down_added", "out_done"))

        pool_held, dve_held = sem("pool_held"), sem("dve_held")

        block = ctx.enter_context(nc.Block())

        def wait(eng, s, n):
            if not (isinstance(n, int) and n <= 0):
                eng.wait_ge(s, n)

        def passes(eng, one):
            one("before", -1, -1, -1, -1)
            one("first", 0, 0, 0, 0)
            with eng.Fori(1, NG - 1) as g:
                one("inner", g, g, 0, 0)
            with eng.Fori(0, B - 1) as b:
                one("turn", b * NG + (NG - 1), NG - 1, b, b)
                with eng.Fori(0, NG - 1) as g:
                    it = b * NG + NG + g
                    one("inner", it, g, (it - 1) // NG, b + 1)
            one("last", ITS - 1, NG - 1, B - 1, B - 1)
            one("after", ITS, 0, B - 1, B, slice(0, 2))

        def s_at(it, unit, r):
            return S_PRE + it * S_PER + S_FIRST[unit] + r

        def qk_at(it, head, j):
            return QK_PRE + QK_PER * it + (4 if head == "N" else 0) + j

        def v_at(it, what, i):
            return V_PRE + V_PER * it + (2 + i if what == "VN" else i - 2)

        def qk_bank(j):
            return scores[j // 2][:, chunk_cols(j % 2)]

        def sum_col(unit, r):
            head, c = UNITS[unit]
            return "AB".index(head) * NB + c * CB + r

        def block_of(unit, r):
            qb = UNITS[unit][1] * CB + r
            return qb, (qb + 1) * P

        def score_start(keys):
            return CW // 2 if CW < keys < CW + 2 * P else 0

        def ln_place(kind, before, step):
            made = [s for s in steps_of(kind) if s[0] == "L"].index(step)
            if kind == "before":
                return made, (pj_bank, z_bank, turned[0], turned[1])[made]
            return L_PER * (before + 1) + made, pj_bank

        def tile_cols(unit, kb):
            return max(0, kb - UNITS[unit][1] * CB) * P

        def chunk_cols(c):
            return slice(c * CW, (c + 1) * CW)

        LAG = 2
        LN_APPLY = 6
        STATS_AT, MEAN_AT = (2, 3), 4
        LN_APPLY_AT = (0,)
        LN_AT = 2

        HALF = F - (FT - 1) * P

        def rows(f):
            return slice(P - HALF, P) if f == FT - 1 else slice(0, P)

        def gate_rows(f):
            return slice(0, HALF) if f == FT - 1 else slice(0, P)

        def product_cols(f):
            return slice(0, CW) if f == FT - 1 else slice(CW, 2 * CW)

        def hidden(n, f):
            if f < 4:
                return v[n][:, 2 * f:2 * f + 2, :].rearrange("p a b -> p (a b)")
            return z[n][rows(f), f - 4, 0:CW]

        @block.sync
        def _(sp):
            def load_qkv(g):
                sp.dma_start(raw_qkv[:, :], wqkv[ds(g, 1)].rearrange("a p n -> p (a n)")).then_inc(qkv_in, 16)

            def load_o(g):
                sp.dma_start(raw_o[:, :], wo[ds(g, 1)].rearrange("a p n -> p (a n)")).then_inc(wo_in, 16)

            for c in range(2):
                sp.dma_start(stream[:, c * CB:(c + 1) * CB, :], x_blocks[:, c * CB:(c + 1) * CB, :]).then_inc(x_in[c], 16)
            load_qkv(0)
            for i, w in enumerate((w1, w2)):
                dst = raw_ff[:, i, :].rearrange("p (t f) -> p t f", t=DT)[:, :, 0:F]
                sp.dma_start(dst, w.rearrange("(t p) f -> p t f", p=P)).then_inc(ff_in, 16)
            down = raw_ff[:, 2, :].rearrange("p (t d) -> p t d", t=FT)
            sp.dma_start(down[:, 0:FT - 1, :], w3[0:(FT - 1) * P, :].rearrange("(t p) d -> p t d", p=P)).then_inc(ff_in, 16)
            sp.dma_start(down[rows(FT - 1), FT - 1, :], w3[(FT - 1) * P:F, :]).then_inc(ff_in, 16)
            for b in range(1, B):
                sp.dma_start(stream[:, b * NB:(b + 1) * NB, :], x_blocks[:, b * NB:(b + 1) * NB, :]).then_inc(x_in[2], 16)

            def one(kind, it, g, before, this, part=None):
                if kind in ("before", "after"):
                    return
                wait(sp, w_split, W_PER * it)
                load_o(g)
                if kind != "last":
                    sp.wait_ge(w_split, W_PER * it + 3)
                    load_qkv(0 if kind == "turn" else g + 1)

            passes(sp, one)

            with sp.Fori(0, NCH) as c:
                sp.wait_ge(down_added, 2 * c + 2)
                sp.dma_start(out_blocks[:, ds(c * CB, CB), :], stream[:, ds(c * CB, CB), :]).then_inc(out_done, 16)
            sp.wait_ge(out_done, 16 * NCH)

        @block.gpsimd
        def _(pool):
            gp = nc.gpsimd

            def hold(s, n):
                if not (isinstance(n, int) and n <= 0):
                    pool.wait_ge(s, n)
                    pool.sem_inc(pool_held, 1)

            gp.memset(ident[:, :], 0.0).then_inc(const_made, 1)
            gp.memset(causal[:, :], 0.0).then_inc(const_made, 1)
            gp.memset(minus_half[:, :], -0.5).then_inc(const_made, 1)
            gp.memset(ones[:, :], 1.0).then_inc(const_made, 1)
            pool.wait_ge(const_made, 4)
            gp.affine_select(out=ident[:, :], in_=ident[:, :], compare_op=ALU.not_equal, fill=1.0, base=0,
                             pattern=[[-1, P]], channel_multiplier=1).then_inc(const_made, 1)
            gp.affine_select(out=causal[:, :], in_=causal[:, :], compare_op=ALU.is_ge, fill=MASKED, base=0,
                             pattern=[[-1, P]], channel_multiplier=1).then_inc(const_made, 1)
            for i in range(2):
                gp.memset(raw_ff[:, i, :].rearrange("p (t f) -> p t f", t=DT)[:, :, F:FP], 0.0).then_inc(ff_pad, 1)

            def split(raw, hi, lo, n):
                if n > 0:
                    gp.tensor_copy(hi, raw).then_inc(w_hi, 1)
                hold(w_hi, n + 1)
                gp.tensor_tensor(lo, raw, hi.bitcast(f32), ALU.subtract).then_inc(w_split, 1)

            def flat(t):
                return t[:, :, :].rearrange("p a b -> p (a b)")

            def flat4(t):
                return t[:, :, :, :].rearrange("p a b c -> p (a b c)")

            def split_qk(head, n):
                at = 0 if head == "A" else QKW
                split(raw_qkv[:, at:at + QKW], flat4(w_qk[head, "hi"]), flat4(w_qk[head, "lo"]), n)

            def split_v(n):
                split(raw_qkv[:, 2 * QKW:], flat(w_v["hi"]), flat(w_v["lo"]), n)

            def norm_stats(a, z, count, used):
                hold(ln_mv, count + 1)
                hold(ln_normed, used)
                gp.tensor_scalar(var_eps[:, a:z], mean_var[:, a:z, 1], EPS_LN, None, ALU.add).then_inc(ln_eps, 1)
                hold(ln_eps, count + 1)
                gp.tensor_tensor(rstd[:, a:z], var_eps[:, a:z], minus_half[:, a:z], ALU.pow).then_inc(ln_rstd, 1)

            norm_stats(0, CB, 0, 0)
            norm_stats(CB, NB, 1, 0)
            pool.wait_ge(qkv_in, 16)
            split_qk("A", 0)
            split_v(1)
            split_qk("B", 2)

            def quantise(k):
                i, part = divmod(k, 3)
                dst = (w_up[0], w_up[1], w_down)[i][:, :, :].rearrange("p a b -> p (a b)")
                below = dst.bitcast(f32)
                if part == 0:
                    if i == 0:
                        pool.wait_ge(ff_limit, 2)
                    gp.tensor_scalar(dst, raw_ff[:, i, :], neg_limit[:, i:i + 1], None, ALU.is_lt).then_inc(ff_below, 1)
                elif part == 1:
                    pool.wait_ge(ff_below, i + 1)
                    gp.tensor_scalar(raw_ff[:, i, :], raw_ff[:, i, :], limit[:, i:i + 1], None, ALU.is_gt).then_inc(ff_above, 1)
                else:
                    pool.wait_ge(ff_above, i + 1)
                    gp.tensor_tensor(dst, raw_ff[:, i, :], below, ALU.subtract).then_inc(ff_quant, 1)

            def one(kind, it, g, before, this, part=None):
                if kind in ("before", "after"):
                    return
                for step in steps_of(kind):
                    if step == ("R", "A0"):
                        hold(wo_in, 16 * (it + 1))
                        if kind != "first":
                            hold(pj_done, pj_at(kind, it, ("O", "P1", 1)) + 1)
                        split(raw_o[:, :], flat(w_o["hi"]), flat(w_o["lo"]), W_PER * it + 3)
                        if kind in ("turn", "last"):
                            norm_stats(0, NB, before + 2, (before + 1) * NB)
                        if kind != "last":
                            hold(qkv_in, 16 * (it + 2))
                            hold(qk_done, qk_at(it, "B", 0))
                            split_qk("A", W_PER * (it + 1))
                            hold(pj_done, pj_at(kind, it, ("V", 3)) + 1)
                            split_v(W_PER * (it + 1) + 1)
                            hold(qk_done, qk_at(it, "B", 3) + 1)
                            split_qk("B", W_PER * (it + 1) + 2)
                        if kind == "first":
                            for k in range(9):
                                quantise(k)
                            pool.wait_ge(ff_quant, 3)
                            gp.tensor_copy(w_up[0][:, :, F:FP], w_up[1][:, :, FP - P:F]).then_inc(ff_quant, 1)

            passes(pool, one)

            with pool.Fori(2, NCH) as c:
                norm_stats(0, CB, B + c, NB * B + c * CB)

        @block.scalar
        def _(act):
            sc = nc.scalar

            def one(kind, it, g, before, this, part=slice(None)):
                for step in with_late_exponentials(steps_of(kind))[part]:
                    what = step[0]
                    if what == "S":
                        unit, r = step[1:]
                        at = s_at(it, unit, r)
                        _, keys = block_of(unit, r)
                        if r == 0:
                            wait(act, t_done, T_PER * it + {"A1": 0, "B0": 4, "B1": 12, "N0": 16}[unit])
                        act.wait_ge(s_max, at + 1)
                        col = sum_col(unit, r)
                        start = score_start(keys)
                        sc.activation(probs[UNITS[unit][1]][:, r, 0:keys], scores[r % 2][:, start:start + keys], ACT.Exp,
                                      bias=neg_max[:, col:col + 1], accum_out=row_sum[:, col:col + 1]).then_inc(s_exp, 1)
                    elif what == "T":
                        unit, kb = step[1:]
                        at = T_PER * it + T_FIRST[unit] + kb
                        c0 = tile_cols(unit, kb)
                        i = T_FIRST[unit] + kb
                        wait(act, av_done, at - PT_RING + 1)
                        act.wait_ge(t_done, at + 1)
                        sc.activation(probsT["hi"][:, i % PT_RING, c0:CW], turned[i % 2][:, c0:CW], ACT.Copy).then_inc(t_hi, 1)
                    elif what == "AE":
                        unit = step[1]
                        head, c = UNITS[unit]
                        if kind != "first":
                            act.wait_ge(pj_done, pj_start(kind, it) + (O_PREV if unit == "B1" else 0))
                        act.wait_ge(av_done, T_PER * it + T_FIRST[unit] + TILES[unit])
                        sc.activation(z["hi"][:, "AB".index(head), chunk_cols(c)], z_bank[:, :], ACT.Copy).then_inc(z_hi, 1)
                    elif what in ("V", "VN"):
                        i = step[1]
                        wait(act, av_done, T_PER * it + (T_FIRST["B1"] + 2 * i + 2 if what == "VN" else 0))
                        act.wait_ge(pj_done, pj_at(kind, it, step) + 1)
                        dst = v["hi"][:, 2 * i:2 * i + 2, :].rearrange("p a b -> p (a b)")
                        sc.activation(dst, pj_bank[:, :], ACT.Copy).then_inc(values_hi, 1)
                    elif what == "QK":
                        head, j = step[1:]
                        wait(act, s_done, S_PRE + S_PER * it + (4 if head == "B" else 12))
                        act.wait_ge(qk_done, qk_at(it, head, j) + 1)
                        sc.activation(qk["hi"][:, j % 2, chunk_cols(j // 2)], qk_bank(j), ACT.Copy,
                                      scale=1.0 if j % 2 else SCALE).then_inc(qk_hi, 1)
                    elif what == "L":
                        if step[1] in (0, 1) and kind != "before":
                            act.wait_ge(qk_done, qk_at(it, "B", 1 + 2 * step[1]) + 1)
                            if step[1] == 1:
                                act.wait_ge(pj_done, pj_at(kind, it, ("V", 3)) + 1)
                        n, bank = ln_place(kind, before, step)
                        t, c = divmod(step[1], 2)
                        act.wait_ge(ln_turned, n + 1)
                        sc.activation(xT["hi"][:, t, chunk_cols(c)], bank[:, :], ACT.Copy).then_inc(ln_hi, 1)
                    if kind == "first" and step in FF_SUM_AT:
                        i = FF_SUM_AT.index(step)
                        if i == 0:
                            act.wait_ge(ff_in, 16 * 4)
                            act.wait_ge(ff_pad, 3)
                        sc.activation((w_up[0], w_up[1], w_down)[i][:, :, :].rearrange("p a b -> p (a b)"), raw_ff[:, i, :], ACT.Abs,
                                      accum_out=abs_sum[:, i:i + 1]).then_inc(ff_abs, 1)

            act.wait_ge(qkv_in, 16)
            sc.activation(w_qk["A", "hi"][:, :, :, :].rearrange("p a b c -> p (a b c)"), raw_qkv[:, 0:QKW], ACT.Copy).then_inc(w_hi, 1)
            passes(act, one)

            def ln_chunk(c):
                for t in range(DT):
                    act.wait_ge(ln_turned, L_PER * B + DT * c + t + 1)
                    bank = (pj_bank, z_bank)[t]
                    dst = xT["hi"][:, t, ds((c % 2) * CW, CW)]
                    sc.activation(dst, bank[:, :], ACT.Copy).then_inc(ln_hi, 1)

            def chunk(c, first, last):
                for f in range(FT):
                    at = FT * c + f
                    act.wait_ge(up_done, at + 1)
                    wait(act, hid_done, at - 1)
                    sc.activation(probs[0][rows(f), f % 2, :], scores[f % 2][gate_rows(f), 0:CW], ACT.Sigmoid).then_inc(sig_done, 1)
                    act.wait_ge(hid_done, at + 1)
                    sc.activation(hidden("hi", f), probs[0][rows(f), 2 + f % 2, :], ACT.Copy).then_inc(hid_hi, 1)
                    if f == LN_AT and not (first or last):
                        ln_chunk(c + 1)

            chunk(0, True, False)
            with act.Fori(1, NCH - 1) as c:
                chunk(c, False, False)
            chunk(NCH - 1, False, True)

        @block.vector
        def _(dve):
            ve = nc.vector

            def lo_part(dst, src, hi, done, scale=None):
                if scale is None:
                    ve.tensor_tensor(dst, src, hi.bitcast(f32), ALU.subtract).then_inc(done, 1)
                else:
                    ve.scalar_tensor_tensor(out=dst, in0=src, scalar=scale, in1=hi.bitcast(f32),
                                            op0=ALU.mult, op1=ALU.subtract).then_inc(done, 1)

            def ln_block_stats(first_block, k):
                ve.bn_stats(stats[:, k, :], stream[:, ds(first_block + k, 1), :].rearrange("p a b -> p (a b)")).then_inc(ln_stats, 1)

            def ln_mean_var(a, z, count):
                dve.wait_ge(ln_stats, count)
                dve.sem_inc(dve_held, 1)
                for k in range(a, z):
                    last = ve.bn_aggr(mean_var[:, k, :], stats[:, k, :])
                last.then_inc(ln_mv, 1)

            def ln_apply(first_block, blocks, rstd_count):
                dve.wait_ge(ln_rstd, rstd_count)
                for k in blocks:
                    ve.tensor_scalar(normed[:, k, :], stream[:, ds(first_block + k, 1), :].rearrange("p a b -> p (a b)"),
                                     mean_var[:, k, 0:1], rstd[:, k:k + 1], ALU.subtract, ALU.mult).then_inc(ln_normed, 1)

            def one(kind, it, g, before, this, part=slice(None)):
                next_batch = 0 if kind == "last" else before + 1
                recs = [s[1] for s in PASS if s[0] == "R"]
                for step in steps_of(kind)[part]:
                    if kind == "first" and step == FF_LIMIT_AT:
                        dve.wait_ge(ff_sum, 1)
                        ve.tensor_scalar(limit[:, :], pj_bank[:, 0:3], 0.5 / (F * D), 0.5 * EPS_Q, ALU.mult, ALU.add).then_inc(ff_limit, 1)
                        ve.tensor_scalar(neg_limit[:, :], pj_bank[:, 0:3], -0.5 / (F * D), -0.5 * EPS_Q, ALU.mult, ALU.add).then_inc(ff_limit, 1)
                    what = step[0]
                    if what == "S":
                        unit, r = step[1:]
                        at = s_at(it, unit, r)
                        _, keys = block_of(unit, r)
                        start = score_start(keys)
                        tile = scores[r % 2][:, start:start + keys]
                        diag = tile[:, keys - P:keys]
                        dve.wait_ge(s_done, at + 1)
                        ve.tensor_tensor(diag, diag, causal[:, :], ALU.add).then_inc(s_masked, 1)
                        dve.wait_ge(s_masked, at + 1)
                        col = sum_col(unit, r)
                        ve.tensor_reduce(neg_max[:, col:col + 1], tile, AX.X, ALU.max, negate=True).then_inc(s_max, 1)
                    elif what == "R":
                        unit = step[1]
                        col = sum_col(unit, 0)
                        dve.wait_ge(s_exp, S_PRE + S_PER * it + CB * ORDER[unit])
                        ve.reciprocal(row_rec[:, col:col + CB], row_sum[:, col:col + CB]).then_inc(s_rec, 1)
                    elif what == "T":
                        unit, kb = step[1:]
                        at = T_PER * it + T_FIRST[unit] + kb
                        c0 = tile_cols(unit, kb)
                        i = T_FIRST[unit] + kb
                        dve.wait_ge(t_hi, at + 1)
                        slot = i % PT_RING
                        lo_part(probsT["lo"][:, slot, c0:CW], turned[i % 2][:, c0:CW], probsT["hi"][:, slot, c0:CW], t_lo)
                        if kind in ("turn", "last") and i < NB // 2:
                            if i == 0:
                                dve.wait_ge(x_in[2], 16 * (B - 1))
                            for k in (2 * i, 2 * i + 1):
                                ln_block_stats(next_batch * NB, k)
                        if kind in ("turn", "last") and i == NB // 2:
                            ln_mean_var(0, NB, (before + 2) * NB)
                        if kind in ("turn", "last") and 0 <= i - LN_APPLY < NB // 2:
                            k = 2 * (i - LN_APPLY)
                            ln_apply(next_batch * NB, (k, k + 1), before + 3)
                    elif what == "AE":
                        unit = step[1]
                        head, c = UNITS[unit]
                        h = "AB".index(head)
                        dve.wait_ge(z_hi, Z_PER * it + ORDER[unit] + 1)
                        lo_part(z["lo"][:, h, chunk_cols(c)], z_bank[:, :], z["hi"][:, h, chunk_cols(c)], z_lo)
                    elif what in ("V", "VN"):
                        i = step[1]
                        dve.wait_ge(values_hi, v_at(it, what, i) + 1)
                        hi, lo = (v[n][:, 2 * i:2 * i + 2, :].rearrange("p a b -> p (a b)") for n in ("hi", "lo"))
                        lo_part(lo, pj_bank[:, :], hi, pj_out)
                    elif what == "QK":
                        head, j = step[1:]
                        dve.wait_ge(qk_hi, qk_at(it, head, j) + 1)
                        cols = chunk_cols(j // 2)
                        lo_part(qk["lo"][:, j % 2, cols], qk_bank(j), qk["hi"][:, j % 2, cols], qk_out,
                                None if j % 2 else SCALE)
                    elif what == "O":
                        unit, i = step[1:]
                        dve.wait_ge(s_rec, R_PER * it + (0 if unit == "P1" else recs.index(unit) + 1))
                        dve.wait_ge(pj_done, pj_at(kind, it, step) + 1)
                        batch = before if unit == "P1" else this
                        for k in range(OB):
                            qb, _ = block_of(unit, OB * i + k)
                            col = sum_col(unit, OB * i + k)
                            dst = stream[:, ds(batch * NB + qb, 1), :].rearrange("p a b -> p (a b)")
                            last = ve.scalar_tensor_tensor(out=dst, in0=pj_bank[:, k * D:(k + 1) * D], scalar=row_rec[:, col:col + 1],
                                                           in1=dst, op0=ALU.mult, op1=ALU.add)
                        last.then_inc(pj_out, 1)
                    elif what == "L":
                        n, bank = ln_place(kind, before, step)
                        t, c = divmod(step[1], 2)
                        dve.wait_ge(ln_hi, n + 1)
                        lo_part(xT["lo"][:, t, chunk_cols(c)], bank[:, :], xT["hi"][:, t, chunk_cols(c)], ln_lo)

            ve.memset(raw_ff[0:P - HALF, 2, (FT - 1) * D:FT * D], 0.0).then_inc(ff_pad, 1)
            for c in range(2):
                dve.wait_ge(x_in[c], 16)
                for k in range(c * CB, (c + 1) * CB):
                    ln_block_stats(0, k)
                ln_mean_var(c * CB, (c + 1) * CB, (c + 1) * CB)
            ln_apply(0, range(CB), 1)
            ln_apply(0, range(CB, NB), 2)
            dve.wait_ge(const_made, 6)
            passes(dve, one)

            def ln_chunk(c):
                for t in range(DT):
                    dve.wait_ge(ln_hi, L_PER * B + DT * c + t + 1)
                    bank = (pj_bank, z_bank)[t]
                    cols = ds((c % 2) * CW, CW)
                    lo_part(xT["lo"][:, t, cols], bank[:, :], xT["hi"][:, t, cols], ln_lo)

            def add_down(c):
                for i in range(2):
                    dve.wait_ge(down_done, c + 1)
                    dst = stream[:, ds(c * CB + 2 * i, 2), :].rearrange("p a b -> p (a b)")
                    ve.tensor_tensor(dst, turned[i][:, :], dst, ALU.add).then_inc(down_added, 1)

            def chunk(c, first, last, stats_next):
                ln_next = not (first or last)
                for f in range(FT):
                    at = FT * c + f
                    dve.wait_ge(sig_done, at + 1)
                    wait(dve, hid_hi, at - 1)
                    ve.tensor_tensor(probs[0][rows(f), 2 + f % 2, :], scores[f % 2][rows(f), product_cols(f)],
                                     probs[0][rows(f), f % 2, :], ALU.mult).then_inc(hid_done, 1)
                    if f == LAG - 1 and not first:
                        add_down(c - 1)
                    if first and f in (0, 2):
                        one("after", ITS, 0, B - 1, B, slice(2 + f // 2, 3 + f // 2))
                    if ln_next and f in LN_APPLY_AT:
                        n = CB // len(LN_APPLY_AT)
                        i = LN_APPLY_AT.index(f) * n
                        ln_apply((c + 1) * CB, range(i, i + n), B + c + 2)
                    if f == LN_AT and ln_next:
                        ln_chunk(c + 1)
                    if stats_next and f in STATS_AT:
                        n = CB // len(STATS_AT)
                        i = STATS_AT.index(f) * n
                        for k in range(i, i + n):
                            ln_block_stats((c + 2) * CB, k)
                    if stats_next and f == MEAN_AT:
                        ln_mean_var(0, CB, NB * B + CB * (c + 3))
                    dve.wait_ge(hid_hi, at + 1)
                    lo_part(hidden("lo", f), probs[0][rows(f), 2 + f % 2, :], hidden("hi", f), hid_lo)

            chunk(0, True, False, True)
            with dve.Fori(1, NCH - 2) as c:
                chunk(c, False, False, True)
            chunk(NCH - 2, False, False, False)
            chunk(NCH - 1, False, True, False)
            add_down(NCH - 1)

        @block.tensor
        def _(pe):
            te = nc.tensor

            def product(dst, pairs):
                todo = [(a(m), b(n)) for a, b in pairs for m, n in (("hi", "hi"), ("hi", "lo"), ("lo", "hi"))]
                for k, (a, b) in enumerate(todo):
                    last = te.matmul(dst, a, b, start=k == 0, stop=k == len(todo) - 1)
                return last

            def av_lo(it, unit, kb):
                i = T_FIRST[unit] + kb
                c0 = tile_cols(unit, kb)
                h = "AB".index(UNITS[unit][0])
                pe.wait_ge(t_lo, T_PER * it + i + 1)
                te.matmul(z_bank[:, c0:CW], v["hi"][:, kb, h * DH:(h + 1) * DH], probsT["lo"][:, i % PT_RING, c0:CW],
                          start=False, stop=kb == TILES[unit] - 1).then_inc(av_done, 1)

            def pj_bank_free(kind, it, before, step):
                steps = steps_of(kind)
                users = [s for s in steps[:steps.index(step)] if s[0] in ("V", "VN", "O", "L")]
                if users and users[-1][0] == "L":
                    pe.wait_ge(ln_lo, ln_place(kind, before, users[-1])[0] + 1)
                else:
                    wait(pe, pj_out, pj_at(kind, it, step))

            def one(kind, it, g, before, this, part=slice(None)):
                for step in steps_of(kind)[part]:
                    if kind == "first" and step == FF_LIMIT_AT:
                        pe.wait_ge(ff_abs, 3)
                        pe.wait_ge(pj_out, pj_at(kind, it, FF_LIMIT_AFTER) + 1)
                        te.matmul(pj_bank[:, 0:3], ones[:, :], abs_sum[:, :], start=True, stop=True).then_inc(ff_sum, 1)
                    what = step[0]
                    if what == "S":
                        unit, r = step[1:]
                        at = s_at(it, unit, r)
                        qb, keys = block_of(unit, r)
                        wait(pe, s_exp, at - 1)
                        if r == 0 and unit in ("B0", "N0"):
                            pe.wait_ge(qk_out, qk_at(it, "B" if unit == "B0" else "N", 3) + 1)
                        start = score_start(keys)
                        for bank in range(0, start + keys, CW):
                            c0, c1 = max(start, bank), min(start + keys, bank + CW)
                            last = product(scores[r % 2][:, c0:c1],
                                           [(lambda n: qk[n][:, 0, qb * P:(qb + 1) * P], lambda n: qk[n][:, 1, c0 - start:c1 - start])])
                        last.then_inc(s_done, 1)
                    elif what == "T":
                        unit, kb = step[1:]
                        i = T_FIRST[unit] + kb
                        at = T_PER * it + i
                        wait(pe, t_lo, at - 1)
                        if kb == 0:
                            pe.wait_ge(s_exp, S_PRE + S_PER * it + {"A0": 0, "A1": 4, "B0": 8, "B1": 12}[unit])
                        c0 = tile_cols(unit, kb)
                        for r in range(c0 // P, CB):
                            src = probs[UNITS[unit][1]][:, r, kb * P:(kb + 1) * P]
                            last = te.transpose(turned[i % 2][:, r * P:(r + 1) * P], src, ident[:, :])
                        last.then_inc(t_done, 1)
                    elif what == "AV":
                        unit, kb = step[1:]
                        head, c = UNITS[unit]
                        i = T_FIRST[unit] + kb
                        at = T_PER * it + i
                        if kb == 0:
                            wait(pe, z_lo, Z_PER * it + ORDER[unit])
                            if unit == "A0":
                                pe.wait_ge(pj_out, pj_start(kind, it))
                        if unit == "A1" and kb in (4, 6):
                            pe.wait_ge(pj_out, pj_at(kind, it, ("V", kb // 2)) + 1)
                        if kb > 0:
                            av_lo(it, unit, kb - 1)
                        pe.wait_ge(t_hi, at + 1)
                        c0 = tile_cols(unit, kb)
                        h = "AB".index(head)
                        for m in ("hi", "lo"):
                            te.matmul(z_bank[:, c0:CW], v[m][:, kb, h * DH:(h + 1) * DH], probsT["hi"][:, i % PT_RING, c0:CW],
                                      start=kb == 0 and m == "hi", stop=False)
                    elif what == "AE":
                        av_lo(it, step[1], TILES[step[1]] - 1)
                    elif what in ("V", "VN"):
                        i = step[1]
                        pj_bank_free(kind, it, before, step)
                        if i % 2 == 0:
                            pe.wait_ge(w_split, W_PER * (it + (what == "VN")) + 2)
                        for k in range(2):
                            pb0 = 2 * i + k
                            last = product(pj_bank[:, k * GW:(k + 1) * GW],
                                           [(lambda n, t=t: xT[n][:, t, pb0 * P:(pb0 + 1) * P], lambda n, t=t: w_v[n][:, t, :])
                                            for t in range(DT)])
                        last.then_inc(pj_done, 1)
                    elif what == "QK":
                        head, j = step[1:]
                        wait(pe, s_exp, S_PRE + S_PER * it + (12 if head == "N" else 4) - 1 + j // 2)
                        if j == 0:
                            pe.wait_ge(w_split, W_PER * it + (3 if head == "B" else W_PER + 1))
                        if kind in ("before", "turn") and head == "N" and j % 2 == 0:
                            pe.wait_ge(ln_lo, L_PER * (before + 1) + 2 + j)
                        w = "A" if head == "N" else "B"
                        cols = chunk_cols(j // 2)
                        product(qk_bank(j), [(lambda n, t=t: w_qk[w, n][:, j % 2, t, :], lambda n, t=t: xT[n][:, t, cols])
                                             for t in range(DT)]).then_inc(qk_done, 1)
                    elif what == "O":
                        unit, i = step[1:]
                        pj_bank_free(kind, it, before, step)
                        if kind == "first" and step == FF_LIMIT_BEFORE:
                            pe.wait_ge(ff_limit, 2)
                        if i == 0:
                            z_made = 0 if unit == "P1" else ORDER[unit] + 1
                            pe.wait_ge(z_lo, Z_PER * it + z_made)
                            pe.wait_ge(w_split, W_PER * (it if unit == "P1" else it + 1))
                        h = "AB".index(UNITS[unit][0])
                        for k in range(OB):
                            qb, _ = block_of(unit, OB * i + k)
                            last = product(pj_bank[:, k * D:(k + 1) * D],
                                           [(lambda n: z[n][:, h, qb * P:(qb + 1) * P], lambda n: w_o[n][:, h, :])])
                        last.then_inc(pj_done, 1)
                    elif what == "L":
                        n, bank = ln_place(kind, before, step)
                        t, c = divmod(step[1], 2)
                        if kind != "before":
                            pj_bank_free(kind, it, before, step)
                        if t == 0:
                            pe.wait_ge(ln_normed, NB * (before + 1) + CB * (c + 1))
                        for k in range(CB):
                            last = te.transpose(bank[:, k * P:(k + 1) * P], normed[:, c * CB + k, t * P:(t + 1) * P], ident[:, :])
                        last.then_inc(ln_turned, 1)

            pe.wait_ge(const_made, 6)
            passes(pe, one)

            def ln_chunk(c):
                for t in range(DT):
                    if t == 0:
                        pe.wait_ge(ln_normed, NB * B + CB * (c + 1))
                    pe.wait_ge(ln_lo, L_PER * B + DT * c)
                    for k in range(CB):
                        last = te.transpose((pj_bank, z_bank)[t][:, k * P:(k + 1) * P], normed[:, k, t * P:(t + 1) * P], ident[:, :])
                    last.then_inc(ln_turned, 1)

            def up(c, f):
                at = FT * c + f
                wait(pe, hid_done, at - 1)
                if f == 0:
                    pe.wait_ge(ln_lo, L_PER * (B + 1) if isinstance(c, int) and c == 0 else L_PER * B + DT * (c + 1))
                for u in range(1 if f == FT - 1 else 2):
                    todo = [(t, n) for t in range(DT) for n in ("hi", "lo")]
                    for k, (t, n) in enumerate(todo):
                        last = te.matmul(scores[f % 2][:, u * CW:(u + 1) * CW], w_up[u][:, t, f * P:(f + 1) * P],
                                         xT[n][:, t, ds((c % 2) * CW, CW)], start=k == 0, stop=k == len(todo) - 1)
                last.then_inc(up_done, 1)

            def down(c, f):
                pe.wait_ge(hid_lo, FT * c + f + 1)
                for r in range(CB):
                    if f == 0 and r % 2 == 0:
                        wait(pe, down_added, 2 * c - 1 + r // 2)
                    bank = turned[r // 2]
                    for n in ("hi", "lo"):
                        last = te.matmul(bank[:, (r % 2) * D:(r % 2 + 1) * D], hidden(n, f)[:, r * P:(r + 1) * P], w_down[rows(f), f, :],
                                         start=f == 0 and r % 2 == 0 and n == "hi", stop=f == FT - 1 and n == "lo",
                                         skip_group_check=True)
                if f == FT - 1:
                    last.then_inc(down_done, 1)

            def chunk(c, first, last):
                for f in range(FT):
                    up(c, f)
                    if first and f in (0, 2):
                        one("after", ITS, 0, B - 1, B, slice(2 + f // 2, 3 + f // 2))
                    if f == LN_AT and not (first or last):
                        ln_chunk(c + 1)
                    if f >= LAG:
                        down(c, f - LAG)
                    elif not first:
                        down(c - 1, FT - LAG + f)

            pe.wait_ge(ff_quant, 4)
            chunk(0, True, False)
            with pe.Fori(1, NCH - 1) as c:
                chunk(c, False, False)
            chunk(NCH - 1, False, True)
            for f in range(FT - LAG, FT):
                down(NCH - 1, f)


def kernel(L0_attn_x, L0_attn_W_K, L0_attn_W_Q, L0_attn_W_V, L0_attn_W_O, L0_ffn_w1, L0_ffn_w2, L0_ffn_w3):
    import concourse.bacc as bacc
    from concourse.bass_utils import run_bass_kernel_spmd

    def by_head(w):
        return np.asarray(w).reshape(NG, HG, DH, DT, P).transpose(0, 4, 1, 3, 2)

    q, k, v = by_head(L0_attn_W_Q), by_head(L0_attn_W_K), by_head(L0_attn_W_V)
    qk = np.stack([q, k], axis=3).reshape(NG, P, HG * 2 * DT * DH)
    v = v.transpose(0, 1, 3, 2, 4).reshape(NG, P, DT * GW)
    o = np.asarray(L0_attn_W_O).reshape(D, NG, HG, DH).transpose(1, 3, 2, 0).reshape(NG, P, HG * D)
    arrays = {
        "x": np.ascontiguousarray(L0_attn_x),
        "wqkv": np.ascontiguousarray(np.concatenate([qk, v], axis=2)),
        "wo": np.ascontiguousarray(o),
        "w1": np.ascontiguousarray(np.asarray(L0_ffn_w1).T),
        "w2": np.ascontiguousarray(np.asarray(L0_ffn_w2).T),
        "w3": np.ascontiguousarray(np.asarray(L0_ffn_w3).T),
    }
    nc = bacc.Bacc("TRN2", target_bir_lowering=False, num_devices=1)
    args = [nc.dram_tensor(n, a.shape, mybir.dt.from_np(a.dtype), kind="ExternalInput").ap() for n, a in arrays.items()]
    out = nc.dram_tensor("out", (B, S, D), mybir.dt.float32, kind="ExternalOutput").ap()
    build(nc, *args, out)
    return run_bass_kernel_spmd(nc, [arrays], core_ids=[0]).results[0]["out"]
```
